# Optimizing a Trainium2 kernel written in Bass

```python
import numpy as np
import jax
import jax.numpy as jnp

def _softmax(x, axis=-1):
    return jax.nn.softmax(x, axis=axis)

def _gelu(x):
    return jax.nn.gelu(x, approximate=True)

def _silu(x):
    return jax.nn.silu(x)

def _sigmoid(x):
    return jax.nn.sigmoid(x)

def _layernorm(x, axis=-1, eps=1e-05):
    m = jnp.mean(x, axis=axis, keepdims=True)
    v = jnp.var(x, axis=axis, keepdims=True)
    return (x - m) / jnp.sqrt(v + eps)

def _scatter_add(tgt, idx, src, axis=0):
    return tgt.at[idx].add(src)

def _segment_sum(src, seg, n):
    return jax.ops.segment_sum(src, seg, n)
kernel_name = 'mk_adj_preln_d2_adj_r2_16b2fa'

def setup_inputs(seed: int=0):
    np.random.seed(seed)
    _w = jnp.asarray

    def _rec_inputs():
        import jax
        import jax.numpy as jnp
        _gk = jax.random.key(seed)
        x = 0.0002141 + 1 * jax.random.normal(jax.random.fold_in(_gk, 1), (4096, 64), jnp.float32)
        _a = jax.random.bernoulli(jax.random.fold_in(_gk, 2), 0.00195312, (4096, 4096))
        adj = _a.astype(jnp.int32)
        return (x, adj)
    x, adj = _rec_inputs()

    def _L0_gnn_setup():
        import jax, jax.numpy as jnp
        import numpy as np
        N = 6144
        IN_C = 64
        OUT_C = 64
        NEG_INF = -1000000000.0
        key = jax.random.key(seed)
        k1, k2, k3, k4 = jax.random.split(key, 4)
        x = jax.random.normal(k1, (N, IN_C), dtype=jnp.float32)
        edge_index = jax.random.randint(k2, (N, N), 0, 2, dtype=jnp.int32)
        weight_w = jax.random.normal(k3, (IN_C, OUT_C), dtype=jnp.float32) * (1.0 / np.sqrt(IN_C))
        weight_a = jax.random.normal(k4, (2 * OUT_C, 1), dtype=jnp.float32) * (1.0 / np.sqrt(OUT_C))
        bias = jnp.zeros((OUT_C,), dtype=jnp.float32)
        return {'x': x, 'edge_index': edge_index, 'weight_w': weight_w, 'weight_a': weight_a, 'bias': bias}
    _L0_gnn_all = _L0_gnn_setup()
    _L0_gnn_in = {k: v for k, v in _L0_gnn_all.items() if k in ('weight_w', 'weight_a', 'bias')}
    del _L0_gnn_all

    def _L1_gnn_setup():
        import jax, jax.numpy as jnp
        import numpy as np
        N = 2048
        C = 64
        GDEP = 2
        HID = 32
        ALPHA = 0.2
        NEG_INF = jnp.float32(-9000000000000000.0)

        def _gat_layer(h, adj_mask, W_l, lw, lb, a):
            Wh = h @ W_l
            L1, L2 = (lw[:C], lw[C:])
            u = Wh @ L1 @ a
            v = Wh @ L2 @ a
            c = lb @ a
            e = jax.nn.leaky_relu(u + v.T + c, negative_slope=ALPHA)
            scores = jnp.where(adj_mask, e, NEG_INF)
            att = jax.nn.softmax(scores, axis=1)
            return jax.nn.elu(att @ Wh)
        key = jax.random.key(seed)
        ks = jax.random.split(key, 8)
        x = jax.random.normal(ks[0], (N, C), jnp.float32)
        adj = jax.random.randint(ks[1], (N, N), 0, 2, jnp.int32)
        W = jax.random.normal(ks[2], (GDEP, C, C), jnp.float32) / np.sqrt(C)
        lin_w = jax.random.normal(ks[3], (GDEP, 2 * C, HID), jnp.float32) / np.sqrt(2 * C)
        lin_b = jnp.zeros((GDEP, HID), jnp.float32)
        attn = jax.random.normal(ks[4], (GDEP, HID, 1), jnp.float32) / np.sqrt(HID)
        mlp_w = jax.random.normal(ks[5], ((GDEP + 1) * C, C), jnp.float32) / np.sqrt((GDEP + 1) * C)
        mlp_b = jnp.zeros((C,), jnp.float32)
        return dict(x=x, adj=adj, W=W, lin_w=lin_w, lin_b=lin_b, attn=attn, mlp_w=mlp_w, mlp_b=mlp_b)
    _L1_gnn_all = _L1_gnn_setup()
    _L1_gnn_in = {k: v for k, v in _L1_gnn_all.items() if k in ('W', 'lin_w', 'lin_b', 'attn', 'mlp_w', 'mlp_b')}
    del _L1_gnn_all
    return {'x': x, 'adj': adj, 'L0_gnn_weight_w': _L0_gnn_in['weight_w'], 'L0_gnn_weight_a': _L0_gnn_in['weight_a'], 'L0_gnn_bias': _L0_gnn_in['bias'], 'L1_gnn_W': _L1_gnn_in['W'], 'L1_gnn_lin_w': _L1_gnn_in['lin_w'], 'L1_gnn_lin_b': _L1_gnn_in['lin_b'], 'L1_gnn_attn': _L1_gnn_in['attn'], 'L1_gnn_mlp_w': _L1_gnn_in['mlp_w'], 'L1_gnn_mlp_b': _L1_gnn_in['mlp_b']}

def reference(x, adj, L0_gnn_weight_w, L0_gnn_weight_a, L0_gnn_bias, L1_gnn_W, L1_gnn_lin_w, L1_gnn_lin_b, L1_gnn_attn, L1_gnn_mlp_w, L1_gnn_mlp_b):
    import jax
    import jax.numpy as jnp

    def _L0_gnn_ref(x, edge_index, weight_w, weight_a, bias):
        import jax, jax.numpy as jnp
        import numpy as np
        N = 6144
        IN_C = 64
        OUT_C = 64
        NEG_INF = -1000000000.0
        wh = x @ weight_w
        a_src = weight_a[:OUT_C, 0]
        a_dst = weight_a[OUT_C:, 0]
        e = (wh @ a_src)[:, None] + (wh @ a_dst)[None, :]
        e = jax.nn.leaky_relu(e, negative_slope=0.01)
        scores = jnp.where(edge_index > 0, e, NEG_INF)
        attention = jax.nn.softmax(scores, axis=1)
        out = attention @ wh
        return out + bias

    def _L1_gnn_ref(x, adj, W, lin_w, lin_b, attn, mlp_w, mlp_b):
        import jax, jax.numpy as jnp
        import numpy as np
        N = 2048
        C = 64
        GDEP = 2
        HID = 32
        ALPHA = 0.2
        NEG_INF = jnp.float32(-9000000000000000.0)

        def _gat_layer(h, adj_mask, W_l, lw, lb, a):
            Wh = h @ W_l
            L1, L2 = (lw[:C], lw[C:])
            u = Wh @ L1 @ a
            v = Wh @ L2 @ a
            c = lb @ a
            e = jax.nn.leaky_relu(u + v.T + c, negative_slope=ALPHA)
            scores = jnp.where(adj_mask, e, NEG_INF)
            att = jax.nn.softmax(scores, axis=1)
            return jax.nn.elu(att @ Wh)
        mask = adj > 0
        h = x
        outs = [h]
        for i in range(GDEP):
            h = ALPHA * x + (1.0 - ALPHA) * _gat_layer(h, mask, W[i], lin_w[i], lin_b[i], attn[i])
            outs.append(h)
        ho = jnp.concatenate(outs, axis=-1)
        return ho @ mlp_w + mlp_b
    h = jnp.maximum(_layernorm(x, axis=-1), 0.0)
    x = x + _L0_gnn_ref(h, adj, L0_gnn_weight_w, L0_gnn_weight_a, L0_gnn_bias)
    h = jnp.maximum(_layernorm(x, axis=-1), 0.0)
    x = x + _L1_gnn_ref(h, adj, L1_gnn_W, L1_gnn_lin_w, L1_gnn_lin_b, L1_gnn_attn, L1_gnn_mlp_w, L1_gnn_mlp_b)
    return x

_drawn_inputs = setup_inputs


def setup_inputs(seed=0):
    import zlib

    import numpy as np

    out = dict(_drawn_inputs(seed))
    spreads = {'L0_gnn_bias': (0.0, 0.1), 'L1_gnn_lin_b': (0.0, 0.8), 'L1_gnn_mlp_b': (0.0, 0.1)}
    factors = {'L1_gnn_lin_w': 2.978, 'L1_gnn_attn': 2.914}
    for name, (base, spread) in spreads.items():
        noise = np.random.default_rng([zlib.crc32(name.encode()), seed]).standard_normal(out[name].shape)
        drawn = base * np.exp(spread * noise) if base else spread * noise
        out[name] = jnp.asarray(drawn.astype(out[name].dtype))
    for name, factor in factors.items():
        out[name] = (out[name] * factor).astype(out[name].dtype)
    return out
```

```python
from contextlib import ExitStack

import concourse.bass as bass
from concourse import mybir

F32 = mybir.dt.float32
BF16 = mybir.dt.bfloat16
FP8 = mybir.dt.float8e4
U8 = mybir.dt.uint8
I8 = mybir.dt.int8
U32 = mybir.dt.uint32
I32 = mybir.dt.int32
ALU = mybir.AluOpType
ACT = mybir.ActivationFunctionType
AX = mybir.AxisListType

P = 128
N = 4096
C = 64
E1 = C + 1
HID = 32
T = N // P
BT = 4
BW = BT * P
NB = T // BT
GT = 4
NG = T // GT
GW = GT * BW // 4
PARTS = 3
TSLOTS = 4
STAGES = 4
LAYERS = 3
ALPHA = (0.01, 0.2, 0.2)
SLOTS = (4, 8, 8)
SHIFT = 60.0
EPS = 1e-5
MIX = 0.2
BIT = (0x20, 0x10)
ACT_TILES = ((3, 3), (3, 2), (3, 2))
DVE_AT = (3, 6, 6)
PE_TURN_AT = (5, 5, 5)
PE_PROJ_AT = (6, 6, 6)
ACT_EXP_AT, ACT_TURN_AT, ACT_PROJ_AT = 6, 6, 7


def build(nc, x, adj, bias0, mlp_b, w, wT, a0, lT, attn, lin_b, mlp_w, out):
    x_v = x.rearrange("(p t) c -> p t c", t=T)
    out_v = out.rearrange("(p t) c -> p t c", t=T)

    with ExitStack() as ctx:
        def sb(name, shape, dt):
            return ctx.enter_context(nc.sbuf_tensor(name, shape, dt))

        def sem(name):
            return ctx.enter_context(nc.semaphore(name))

        mask = sb("mask", [P, NB // 2, NG * GW], U32)
        room = sb("room", [P, 8 * 2 * GW + STAGES * 4 * GW - 4 * 2 * GW], U32)
        signs = sb("signs", [P, TSLOTS, GW], U32)
        oddbits = sb("oddbits", [P, GW], U32)
        U = sb("U", [P, N], F32)
        Y = sb("Y", [P, T, 2 * PARTS * E1], BF16)
        Wh = sb("Wh", [P, T, E1], F32)
        X = sb("X", [P, T, C], F32)
        H = sb("H", [P, T, C], F32)
        yf = sb("yf", [P, 2, GT, 2, E1], F32)
        S = sb("S", [P, BT, 2, E1], F32)
        num = sb("num", [P, BT, E1], F32)
        num2 = sb("num2", [P, BT, E1], F32)
        hn = sb("hn", [P, 2, BT, C], F32)
        hT = sb("hT", [C, BW], F32)
        vu = sb("vu", [P, T, 2], F32)
        v = sb("v", [P, T], F32)
        nv = sb("nv", [P, T], F32)
        bd = sb("bd", [P, 2, T], F32)
        ac = sb("ac", [P, 2, T], F32)
        z = sb("z", [P, T], F32)
        az = sb("az", [P, T], F32)
        zm = sb("zm", [P, T], F32)
        vmax = sb("vmax", [P, 1], F32)
        vtop = sb("vtop", [1, 1], F32)
        V = sb("V", [P, 1], F32)
        whsum = sb("whsum", [P, E1], F32)
        mean = sb("mean", [P, E1], F32)
        small = sb("small", [P, 4, T], F32)
        half = sb("half", [P, T], F32)
        ident = sb("ident", [P, P], F32)
        ones = sb("ones", [P, P], F32)
        bias_sb = sb("bias_sb", [P, C], F32)
        mlpb_sb = sb("mlpb_sb", [P, C], F32)
        rhs = sb("rhs", [C, LAYERS, C + 2], F32)
        wub = sb("wub", [C, LAYERS, P], F32)
        avu = sb("avu", [C, LAYERS, 2], F32)
        attn_sb = sb("attn_sb", [HID, 2], F32)
        linb_sb = sb("linb_sb", [HID, 2], F32)
        mlp_sb = sb("mlp_sb", [C, LAYERS, C], F32)
        cc = sb("cc", [P, LAYERS], F32)
        ps = ctx.enter_context(nc.psum_tensor("ps", [P, 2, BT, 512], F32))

        params_in = sem("params_in")
        x_in = [sem("x_in0"), sem("x_in1")]
        adj_in = [sem(f"adj_in{s}") for s in range(STAGES)]
        stored = sem("stored")
        const_ready = sem("const_ready")
        cleared = sem("cleared")
        prep_psum = sem("prep_psum")
        prep_copied = sem("prep_copied")
        dve_step = sem("dve_step")
        var_ready = sem("var_ready")
        rstd_ready = sem("rstd_ready")
        centred = sem("centred")
        squared = sem("squared")
        stage_read = sem("stage_read")
        edges_ready = sem("edges_ready")
        act_signs = sem("act_signs")
        dve_signs = sem("dve_signs")
        neg_ready = sem("neg_ready")
        pos_ready = sem("pos_ready")
        bits_used = sem("bits_used")
        elu_in = sem("elu_in")
        elu_exp = sem("elu_exp")
        h_ready = sem("h_ready")
        turned = sem("turned")
        hT_ready = sem("hT_ready")
        projected = sem("projected")
        wh_ready = sem("wh_ready")
        x_added = sem("x_added")
        x_biased = sem("x_biased")
        part_max = sem("part_max")
        part_max_row = sem("part_max_row")
        top_ready = sem("top_ready")
        top_spread = sem("top_spread")
        exps_in = sem("exps_in")
        bd_ready = sem("bd_ready")
        ac_ready = sem("ac_ready")
        y_product = sem("y_product")
        y_high = sem("y_high")
        y_rest = sem("y_rest")
        y_mid = sem("y_mid")
        y_ready = sem("y_ready")
        whsum_ready = sem("whsum_ready")
        mean_psum = sem("mean_psum")
        mean_ready = sem("mean_ready")

        pe_passed = sem("pe_passed")
        act_passed = sem("act_passed")
        dve_passed = sem("dve_passed")

        def slot(s, which):
            return room[:, (2 * s + which) * GW:(2 * s + which + 1) * GW]

        def weights(s, which, j, i):
            at = (j * BT + i) * P
            return slot(s, which).bitcast(FP8)[:, at:at + P]

        def stage(q):
            at = 4 * 2 * GW + q * 4 * GW
            return room[:, at:at + 4 * GW].bitcast(I32)

        def edges(pair, g):
            return mask[:, bass.ds(pair, 1), g * GW:(g + 1) * GW].rearrange("p o w -> p (o w)")

        def urow(pair, u):
            return U[:, bass.ds((2 * pair + u) * BW, BW)]

        def tiles(t, pair, u):
            return t[:, bass.ds((2 * pair + u) * BT, BT)]

        def parts(g0, g1, part):
            return Y[:, g0:g1, :].rearrange("p t (g k c) -> p t g k c", g=2, k=PARTS)[:, :, :, part, :]

        prep = signs[:, :, :].rearrange("p s w -> p (s w)").bitcast(F32)
        wT_sb = prep[0:C, 0:LAYERS * C].rearrange("p (l c) -> p l c", l=LAYERS)
        lT_sb = prep[0:HID, 256:512].rearrange("p (l k c) -> p l k c", l=2, k=2)
        linb_w = prep[0:HID, 512:768].rearrange("p (l c) -> p l c", l=2)

        share = yf[:, :, :, :, :].rearrange("p s t k c -> p (s t k c)")[:, 0:2 * BT * C].rearrange(
            "p (s t c) -> p s t c", s=2, t=BT)

        def squares(t):
            return Y[:, t, 0:2 * C].bitcast(F32)

        def yhat(j, which):
            return Y[:, j, which * PARTS * E1:(which + 1) * PARTS * E1]

        def wide(ap, n):
            return ap.rearrange("p (t o) -> p t o", o=1).broadcast_to([P, ap.shape[1], n])

        def bank(u, b):
            return ps[:, u, b, :]

        def blocks(eng, body):
            body(0, 0)
            body(0, 1)
            with eng.Fori(1, NB // 2) as pair:
                body(pair, 0)
                body(pair, 1)

        def before(pair, u):
            return (pair, 0) if u else (pair - 1, 1)

        def epi(layer, pair, u):
            return (2 * pair + u) + NB * (layer + 1)

        def unit(layer, pair, u, g):
            return (2 * pair + u) * NG + g + layer * NB * NG

        block = ctx.enter_context(nc.Block())

        @block.sync
        def _(sp):
            sp.dma_start(X[:, 0:T // 2, :], x_v[:, 0:T // 2, :]).then_inc(x_in[0], 16)
            sp.dma_start(X[:, T // 2:T, :], x_v[:, T // 2:T, :]).then_inc(x_in[1], 16)
            sp.dma_start(rhs[:, :, 0:C], w).then_inc(params_in, 16)
            sp.dma_start(wT_sb[:, :, :], wT).then_inc(params_in, 16)
            sp.dma_start(avu[:, 0, :], a0).then_inc(params_in, 16)
            sp.dma_start(lT_sb[:, :, :, :], lT).then_inc(params_in, 16)
            sp.dma_start(attn_sb[:, :], attn).then_inc(params_in, 16)
            sp.dma_start(linb_sb[:, :], lin_b).then_inc(params_in, 16)
            sp.dma_start(mlp_sb[:, :, :], mlp_w).then_inc(params_in, 16)
            sp.dma_start(bias_sb[:, :], bias0).then_inc(params_in, 16)
            sp.dma_start(mlpb_sb[:, :], mlp_b).then_inc(params_in, 16)

            def load(pair, u):
                for g in range(NG):
                    G = (2 * pair + u) * NG + g
                    if not (isinstance(pair, int) and G < STAGES):
                        sp.wait_ge(stage_read, G - STAGES + 1)
                    sp.dma_start(stage(g % STAGES), adj[bass.ds(G, 1), :, :].rearrange("o p w -> (o p) w")
                                 ).then_inc(adj_in[g % STAGES], 16)

            blocks(sp, load)

            def store(pair, u):
                sp.wait_ge(x_added, epi(1, pair, u) + 1)
                sp.dma_start(out_v[:, bass.ds((2 * pair + u) * BT, BT), :], tiles(X, pair, u)).then_inc(stored, 16)

            blocks(sp, store)
            sp.wait_ge(stored, 16 * NB)

        @block.tensor
        def _(pe):
            pe.wait_ge(params_in, 16 * 9)
            pe.wait_ge(cleared, 4)
            for l in range(2):
                pe.matmul(bank(0, 0)[0:C, 2 * l:2 * l + 1], lT_sb[:, l, 1, :], attn_sb[:, l:l + 1], start=True, stop=True)
                pe.matmul(bank(0, 0)[0:C, 2 * l + 1:2 * l + 2], lT_sb[:, l, 0, :], attn_sb[:, l:l + 1], start=True, stop=True)
                last = pe.matmul(bank(0, 1)[:, l:l + 1], linb_w[:, l, :], attn_sb[:, l:l + 1], start=True, stop=True)
            last.then_inc(prep_psum, 1)
            pe.wait_ge(prep_copied, 1)
            for l in range(LAYERS):
                last = pe.matmul(bank(0, 2)[0:C, 2 * l:2 * l + 2], wT_sb[:, l, :], avu[:, l, :], start=True, stop=True)
            last.then_inc(prep_psum, 1)
            pe.wait_ge(prep_copied, 2)
            pe.wait_ge(const_ready, 1)

            def turn(layer, pair, u):
                e = epi(layer, pair, u)
                pe.wait_ge(h_ready, e + 1)
                if layer < 0 and pair >= 1:
                    pe.wait_ge(wh_ready, e - 1)
                pe.sem_inc(pe_passed, 1)
                for i in range(BT):
                    h = H[:, (2 * pair + u) * BT + i, :] if layer < 0 else hn[:, u, i, :]
                    last = pe.transpose(bank(u, 0)[0:C, i * P:(i + 1) * P], h, ident[:, :])
                last.then_inc(turned, 1)

            def project(layer, pair, u):
                e = epi(layer, pair, u)
                pe.wait_ge(hT_ready, e + 1)
                for i in range(BT):
                    h = hT[:, i * P:(i + 1) * P]
                    if layer < 2:
                        last = pe.matmul(bank(u, 1)[:, i * (C + 2):(i + 1) * (C + 2)], h, rhs[:, layer + 1, :], start=True, stop=True)
                    if layer >= 0:
                        last = pe.matmul(bank(u, 2)[:, i * C:(i + 1) * C], h, mlp_sb[:, layer, :], start=True, stop=True)
                if layer < 2:
                    last = pe.matmul(bank(u, 3), wub[:, layer + 1, :], hT[:, :], start=True, stop=True)
                last.then_inc(projected, 1)

            for b in range(NB):
                turn(-1, b // 2, b % 2)
                if b:
                    project(-1, (b - 1) // 2, (b - 1) % 2)
            project(-1, NB // 2 - 1, 1)

            for layer in range(LAYERS):
                pe.wait_ge(part_max, layer + 1)
                pe.transpose(bank(1, 0)[0:1, 0:P], vmax[:, :], ident[:, :]).then_inc(part_max_row, 1)
                pe.wait_ge(top_ready, layer + 1)
                pe.matmul(bank(1, 1)[:, 0:1], ones[0:1, :], vtop[:, :], start=True, stop=True).then_inc(top_spread, 1)

                def sums(pair, u, layer=layer):
                    first = isinstance(pair, int)
                    if first and u:
                        pe.wait_ge(mean_ready, layer + 1)
                    if not first:
                        pe.wait_ge(wh_ready, epi(layer, pair, u) - 1)
                    for g in range(NG):
                        G = unit(layer, pair, u, g)
                        if g == PE_TURN_AT[layer] and not (first and not u):
                            turn(layer, *before(pair, u))
                        if g == PE_PROJ_AT[layer] and not (first and not u):
                            project(layer, *before(pair, u))
                        if first and not u:
                            if g == 4:
                                pe.wait_ge(whsum_ready, layer + 1)
                                pe.matmul(bank(1, 2)[:, 0:E1], ones[:, :], whsum[:, :], start=True, stop=True).then_inc(mean_psum, 1)
                            pe.wait_ge(y_ready, layer * NG + g + 1)
                        pe.wait_ge(pos_ready, G + 1)
                        pe.sem_inc(pe_passed, 1)
                        s = g % SLOTS[layer]
                        for jj in range(GT):
                            j = g * GT + jj
                            for i in range(BT):
                                for which in (1, 0):
                                    k = 1 - which
                                    last = pe.matmul(
                                        bank(u, i)[:, k * PARTS * E1:(k + 1) * PARTS * E1],
                                        weights(s, which, jj, i), yhat(j, k),
                                        start=(j == 0 and k == 0), stop=(j == T - 1), skip_group_check=True)
                        last.then_inc(bits_used, 1)

                blocks(pe, sums)
                turn(layer, NB // 2 - 1, 1)
                project(layer, NB // 2 - 1, 1)

        @block.gpsimd
        def _(pool):
            pool.memset(ident[:, :], 0.0).then_inc(cleared, 1)
            pool.memset(ones[:, :], 1.0).then_inc(cleared, 1)
            pool.memset(half[:, :], -0.5).then_inc(cleared, 1)
            pool.wait_ge(cleared, 3)
            pool.affine_select(out=ident[:, :], in_=ident[:, :], compare_op=ALU.not_equal, fill=1.0,
                               base=0, pattern=[[-1, P]], channel_multiplier=1).then_inc(const_ready, 1)

            def rstd(n, a, b):
                pool.wait_ge(var_ready, n + 1)
                pool.tensor_tensor(small[:, 2, a:b], small[:, 1, a:b], half[:, a:b], ALU.pow).then_inc(rstd_ready, 1)

            def all_tiles(t):
                return t[:, :].rearrange("p (o c) -> p o c", o=1).broadcast_to([P, T, C])

            rstd(0, 0, T // 2)
            rstd(1, T // 2, T)
            pool.wait_ge(params_in, 16 * 9)
            pool.tensor_tensor(X[:, :, :], X[:, :, :], all_tiles(bias_sb), ALU.add).then_inc(x_biased, 1)

            for layer in range(LAYERS):
                for g in range(NG):
                    n = layer * NG + g
                    if g == 0:
                        pool.wait_ge(bd_ready, layer + 1)
                        pool.wait_ge(wh_ready, NB * (layer + 1))
                        if layer:
                            pool.wait_ge(x_added, NB * layer)
                    if n >= 2:
                        pool.wait_ge(y_ready, n - 1)
                    t = slice(g * GT, (g + 1) * GT)
                    for k in range(2):
                        last = pool.tensor_tensor(yf[:, g % 2, :, k, :], Wh[:, t, :], wide(bd[:, k, t], E1), ALU.mult)
                    last.then_inc(y_product, 1)

                def add(pair, u, layer=layer):
                    if layer == 0:
                        rstd(2 + (2 * pair + u), 0, BT)
                    pool.wait_ge(wh_ready, epi(layer, pair, u) + 1)
                    pool.tensor_tensor(tiles(X, pair, u), tiles(X, pair, u), share[:, u, :, :], ALU.add).then_inc(x_added, 1)

                if layer == 1:
                    pool.wait_ge(x_added, NB)
                    pool.tensor_tensor(X[:, :, :], X[:, :, :], all_tiles(mlpb_sb), ALU.add).then_inc(x_biased, 1)
                    pool.wait_ge(x_biased, 2)
                blocks(pool, add)

        @block.scalar
        def _(act):
            def turn_out(layer, pair, u):
                e = epi(layer, pair, u)
                act.wait_ge(turned, e + 1)
                if not (layer < 0 and isinstance(pair, int) and pair == 0 and u == 0):
                    act.wait_ge(projected, e)
                act.copy(hT[:, :], bank(u, 0)[0:C, :]).then_inc(hT_ready, 1)

            def project_out(layer, pair, u):
                act.wait_ge(projected, epi(layer, pair, u) + 1)
                if layer < 2:
                    both = bank(u, 1)[:, 0:BT * (C + 2)].rearrange("p (t c) -> p t c", t=BT)
                    act.copy(tiles(vu, pair, u), both[:, :, C:C + 2])
                    act.copy(tiles(Wh, pair, u)[:, :, 0:C], both[:, :, 0:C])
                    last = act.activation(urow(pair, u), bank(u, 3), ACT.Identity, bias=cc[:, layer + 1:layer + 2])
                if layer >= 0:
                    if not (layer == 0 and isinstance(pair, int) and pair == 0):
                        act.wait_ge(x_added, epi(layer - 1, pair, u) - 1)
                    last = act.copy(share[:, u, :, :], bank(u, 2)[:, 0:BT * C].rearrange("p (t c) -> p t c", t=BT))
                last.then_inc(wh_ready, 1)

            act.wait_ge(centred, 1)
            for n in range(2):
                act.wait_ge(centred, n + 1)
                t = slice(n * T // 2, (n + 1) * T // 2)
                act.activation(squares(t), H[:, t, :], ACT.Square).then_inc(squared, 1)
            act.wait_ge(prep_copied, 2)
            for b in range(NB):
                turn_out(-1, b // 2, b % 2)
                if b:
                    project_out(-1, (b - 1) // 2, (b - 1) % 2)
            project_out(-1, NB // 2 - 1, 1)

            for layer in range(LAYERS):
                act.wait_ge(exps_in, 2 * layer + 1)
                act.activation(bd[:, :, :], bd[:, :, :], ACT.Exp).then_inc(bd_ready, 1)
                act.wait_ge(exps_in, 2 * layer + 2)
                act.activation(ac[:, :, :], ac[:, :, :], ACT.Exp).then_inc(ac_ready, 1)

                def signs_of(pair, u, layer=layer):
                    first = isinstance(pair, int)
                    for g in range(NG):
                        G = unit(layer, pair, u, g)
                        n = layer * NG + g
                        if first and not u:
                            act.wait_ge(y_product, n + 1)
                            act.copy(parts(g * GT, (g + 1) * GT, 0), yf[:, g % 2, :, :, :]).then_inc(y_high, 1)
                        if not (first and not u and g < TSLOTS and layer == 0):
                            act.wait_ge(neg_ready, G - TSLOTS + 1)
                        act.sem_inc(act_passed, 1)
                        s8 = signs[:, g % TSLOTS, :].bitcast(I8)
                        for jj in range(ACT_TILES[layer][g % 2]):
                            j = g * GT + jj
                            last = act.activation(s8[:, jj * BW:(jj + 1) * BW], urow(pair, u), ACT.Sign, bias=v[:, j:j + 1])
                        last.then_inc(act_signs, 1)
                        if first and not u:
                            act.wait_ge(y_rest, n + 1)
                            act.copy(parts(g * GT, (g + 1) * GT, 1), yf[:, g % 2, :, :, :]).then_inc(y_mid, 1)
                            continue
                        if layer and g == ACT_EXP_AT:
                            elu(*before(pair, u))
                        if g == ACT_TURN_AT:
                            turn_out(layer, *before(pair, u))
                        if g == ACT_PROJ_AT:
                            project_out(layer, *before(pair, u))

                def elu(pair, u, layer=layer):
                    act.wait_ge(elu_in, (2 * pair + u) + (layer - 1) * NB + 1)
                    act.activation(S[:, :, 0, 0:C], num2[:, :, 0:C], ACT.Exp).then_inc(elu_exp, 1)

                blocks(act, signs_of)
                if layer:
                    elu(NB // 2 - 1, 1)
                turn_out(layer, NB // 2 - 1, 1)
                project_out(layer, NB // 2 - 1, 1)

        @block.vector
        def _(dve):
            chain = [0]

            def link(ins):
                chain[0] += 1
                ins.then_inc(dve_step, 1)
                dve.wait_ge(dve_step, chain[0])

            def steps(base, per, pair, u):
                at = [0]

                def step(ins):
                    at[0] += 1
                    assert at[0] <= per
                    ins.then_inc(dve_step, 1)
                    dve.wait_ge(dve_step, (2 * pair + u) * per + (base + at[0]))
                return step, at

            link(dve.memset(Wh[:, :, C:E1], 1.0))
            link(dve.memset(cc[:, 0:1], 0.0))

            halves = [slice(0, T // 2), slice(T // 2, T)]
            for n, t in enumerate(halves):
                dve.wait_ge(x_in[n], 16)
                link(dve.tensor_reduce(small[:, 0, t], X[:, t, :], AX.X, ALU.add))
                link(dve.tensor_scalar(small[:, 0, t], small[:, 0, t], 1.0 / C, None, ALU.mult))
                dve.tensor_tensor(H[:, t, :], X[:, t, :], wide(small[:, 0, t], C), ALU.subtract).then_inc(centred, 1)
            for n, t in enumerate(halves):
                dve.wait_ge(squared, n + 1)
                link(dve.tensor_reduce(small[:, 1, t], squares(t), AX.X, ALU.add))
                dve.tensor_scalar(small[:, 1, t], small[:, 1, t], 1.0 / C, EPS, ALU.mult, ALU.add).then_inc(var_ready, 1)
            for n, t in enumerate(halves):
                dve.wait_ge(rstd_ready, n + 1)
                link(dve.tensor_tensor(H[:, t, :], H[:, t, :], wide(small[:, 2, t], C), ALU.mult))
                dve.tensor_scalar(H[:, t, :], H[:, t, :], 0.0, None, ALU.max).then_inc(h_ready, NB // 2)

            dve.wait_ge(params_in, 16 * 9)
            dve.wait_ge(cleared, 3)
            for l in range(2):
                last = dve.tensor_scalar(linb_w[:, l, :], ones[0:HID, :], linb_sb[:, l:l + 1], None, ALU.mult)
            last.then_inc(cleared, 1)
            dve.wait_ge(prep_psum, 1)
            dve.tensor_copy(avu[:, 1:3, :], bank(0, 0)[0:C, 0:4].rearrange("p (l k) -> p l k", l=2))
            dve.tensor_copy(cc[:, 1:3], bank(0, 1)[:, 0:2]).then_inc(prep_copied, 1)
            dve.wait_ge(prep_psum, 2)
            link(dve.tensor_copy(rhs[:, :, C:C + 2], bank(0, 2)[0:C, 0:6].rearrange("p (l k) -> p l k", l=LAYERS)))
            for l in range(LAYERS):
                last = dve.tensor_scalar(wub[:, l, :], ones[0:C, :], rhs[:, l, C + 1:C + 2], None, ALU.mult)
            last.then_inc(prep_copied, 1)

            for layer in range(LAYERS):
                alpha = ALPHA[layer]
                dve.wait_ge(wh_ready, NB * (layer + 1))
                dve.reduce_max(vmax[:, :], vu[:, :, 0], AX.X).then_inc(part_max, 1)
                dve.tensor_copy(v[:, :], vu[:, :, 0])
                dve.tensor_scalar(nv[:, :], vu[:, :, 0], -1.0, None, ALU.mult)
                dve.wait_ge(part_max_row, layer + 1)
                dve.reduce_max(vtop[:, :], bank(1, 0)[0:1, 0:P], AX.X).then_inc(top_ready, 1)
                dve.wait_ge(top_spread, layer + 1)
                link(dve.tensor_copy(V[:, :], bank(1, 1)[:, 0:1]))
                dve.tensor_scalar(bd[:, 0, :], vu[:, :, 0], V[:, :], SHIFT, ALU.subtract, ALU.add)
                link(dve.tensor_scalar(bd[:, 1, :], vu[:, :, 0], V[:, :], alpha, ALU.subtract, ALU.mult))
                dve.tensor_scalar(bd[:, 1, :], bd[:, 1, :], SHIFT, None, ALU.add).then_inc(exps_in, 1)
                link(dve.tensor_scalar(z[:, :], vu[:, :, 1], cc[:, layer:layer + 1], V[:, :], ALU.add, ALU.add))
                link(dve.tensor_scalar(az[:, :], z[:, :], alpha, None, ALU.mult))
                link(dve.tensor_tensor(zm[:, :], z[:, :], az[:, :], ALU.max))
                dve.tensor_tensor(ac[:, 0, :], z[:, :], zm[:, :], ALU.subtract)
                dve.tensor_tensor(ac[:, 1, :], az[:, :], zm[:, :], ALU.subtract).then_inc(exps_in, 1)

                base = chain[0]
                per = 15 if layer == 0 else 9

                def epilogue(pair, u, layer=layer, base=base, per=per):
                    step, at = steps(base, per, pair, u)
                    dve.wait_ge(bits_used, unit(layer, pair, u, NG - 1) + 1)
                    dve.wait_ge(ac_ready, layer + 1)
                    dve.wait_ge(mean_ready, layer + 1)
                    for k in range(2):
                        last = dve.tensor_reduce(
                            S[:, :, k, :], ps[:, u, :, k * PARTS * E1:(k + 1) * PARTS * E1].rearrange("p t (q c) -> p t c q", q=PARTS),
                            AX.X, ALU.add)
                    step(last)
                    dve.tensor_tensor(num[:, :, :], S[:, :, 0, :], wide(tiles(ac[:, 0, :], pair, u), E1), ALU.mult)
                    step(dve.tensor_tensor(num2[:, :, :], S[:, :, 1, :], wide(tiles(ac[:, 1, :], pair, u), E1), ALU.mult))
                    step(dve.tensor_tensor(num[:, :, :], num[:, :, :], num2[:, :, :], ALU.add))
                    step(dve.tensor_scalar(small[:, 0, 0:BT], num[:, :, C], 0.0, None, ALU.is_equal))
                    step(dve.tensor_tensor(num2[:, :, :], mean[:, :].rearrange("p (o c) -> p o c", o=1).broadcast_to([P, BT, E1]),
                                           wide(small[:, 0, 0:BT], E1), ALU.mult))
                    step(dve.tensor_tensor(num[:, :, :], num[:, :, :], num2[:, :, :], ALU.add))
                    step(dve.reciprocal(small[:, 3, 0:BT], num[:, :, C]))
                    step(dve.tensor_tensor(num[:, :, 0:C], num[:, :, 0:C], wide(small[:, 3, 0:BT], C), ALU.mult))
                    dve.wait_ge(turned, epi(layer, pair, u) - 1)
                    if layer == 0:
                        dve.wait_ge(x_biased, 1)
                        xt = tiles(X, pair, u)
                        step(dve.tensor_tensor(xt, xt, num[:, :, 0:C], ALU.add))
                        dve.sem_inc(dve_passed, 1)
                        step(dve.tensor_reduce(small[:, 0, 0:BT], xt, AX.X, ALU.add))
                        step(dve.tensor_scalar(small[:, 0, 0:BT], small[:, 0, 0:BT], 1.0 / C, None, ALU.mult))
                        step(dve.tensor_tensor(num[:, :, 0:C], xt, wide(small[:, 0, 0:BT], C), ALU.subtract))
                        step(dve.tensor_tensor(num2[:, :, 0:C], num[:, :, 0:C], num[:, :, 0:C], ALU.mult))
                        step(dve.tensor_reduce(small[:, 1, 0:BT], num2[:, :, 0:C], AX.X, ALU.add))
                        dve.tensor_scalar(small[:, 1, 0:BT], small[:, 1, 0:BT], 1.0 / C, EPS, ALU.mult, ALU.add).then_inc(var_ready, 1)
                        dve.wait_ge(rstd_ready, 2 + (2 * pair + u) + 1)
                        step(dve.tensor_tensor(num[:, :, 0:C], num[:, :, 0:C], wide(small[:, 2, 0:BT], C), ALU.mult))
                        dve.tensor_scalar(hn[:, u, :, :], num[:, :, 0:C], 0.0, None, ALU.max).then_inc(h_ready, 1)
                        dve.wait_ge(h_ready, epi(layer, pair, u) + 1)
                        dve.tensor_scalar(tiles(H, pair, u), hn[:, u, :, :], MIX, MIX - 1.0, ALU.mult, ALU.add)
                    else:
                        n = (2 * pair + u) + (layer - 1) * NB
                        dve.tensor_scalar(num2[:, :, 0:C], num[:, :, 0:C], 0.0, None, ALU.min).then_inc(elu_in, 1)
                        dve.wait_ge(elu_exp, n + 1)
                        step(dve.scalar_tensor_tensor(out=num[:, :, 0:C], in0=num[:, :, 0:C], scalar=0.0, in1=S[:, :, 0, 0:C],
                                                      op0=ALU.max, op1=ALU.add))
                        dve.scalar_tensor_tensor(out=hn[:, u, :, :], in0=num[:, :, 0:C], scalar=1.0 - MIX,
                                                 in1=tiles(H, pair, u), op0=ALU.mult, op1=ALU.add).then_inc(h_ready, 1)
                    assert at[0] == per

                def bits(pair, u, layer=layer, epilogue=epilogue):
                    first = isinstance(pair, int)
                    bit = BIT[u] * 0x01010101
                    for g in range(NG):
                        G = unit(layer, pair, u, g)
                        n = layer * NG + g
                        s = g % SLOTS[layer]
                        if first and not u:
                            dve.wait_ge(y_high, n + 1)
                            dve.tensor_tensor(yf[:, g % 2, :, :, :], yf[:, g % 2, :, :, :], parts(g * GT, (g + 1) * GT, 0),
                                              ALU.subtract).then_inc(y_rest, 1)
                        if layer == 0:
                            dve.wait_ge(adj_in[g % STAGES], (2 * pair + u) * 32 + 16 * (g // STAGES + 1))
                            to = oddbits[:, :] if u else edges(pair, g)
                            dve.tensor_scalar(to.bitcast(U8), stage(g % STAGES), 0.0, float(BIT[u]), ALU.is_gt, ALU.mult
                                              ).then_inc(stage_read, 1)
                            dve.wait_ge(stage_read, G + 1)
                            if u:
                                dve.tensor_tensor(edges(pair, g), edges(pair, g), oddbits[:, :], ALU.bitwise_or).then_inc(edges_ready, 1)
                                dve.wait_ge(edges_ready, pair * NG + (g + 1))
                        s8 = signs[:, g % TSLOTS, :].bitcast(U8)
                        for jj in range(ACT_TILES[layer][g % 2], GT):
                            j = g * GT + jj
                            last = dve.tensor_scalar(s8[:, jj * BW:(jj + 1) * BW], urow(pair, u), nv[:, j:j + 1], float(BIT[0] | BIT[1]),
                                                     ALU.is_lt, ALU.mult)
                        last.then_inc(dve_signs, 1)
                        dve.wait_ge(dve_signs, G + 1)
                        dve.wait_ge(act_signs, G + 1)
                        if not (first and not u and g < SLOTS[layer]):
                            dve.wait_ge(bits_used, G - SLOTS[layer] + 1)
                        dve.scalar_tensor_tensor(out=slot(s, 0), in0=edges(pair, g), scalar=bit, in1=signs[:, g % TSLOTS, :],
                                                 op0=ALU.bitwise_and, op1=ALU.bitwise_and).then_inc(neg_ready, 1)
                        dve.wait_ge(neg_ready, G + 1)
                        dve.scalar_tensor_tensor(out=slot(s, 1), in0=edges(pair, g), scalar=bit, in1=slot(s, 0),
                                                 op0=ALU.bitwise_and, op1=ALU.bitwise_xor).then_inc(pos_ready, 1)
                        if first and not u:
                            dve.wait_ge(y_mid, n + 1)
                            dve.tensor_tensor(parts(g * GT, (g + 1) * GT, 2), yf[:, g % 2, :, :, :], parts(g * GT, (g + 1) * GT, 1),
                                              ALU.subtract).then_inc(y_ready, 1)
                            if g == 1:
                                dve.tensor_reduce(whsum[:, :], Wh[:, :, :].rearrange("p t c -> p c t"), AX.X, ALU.add
                                                  ).then_inc(whsum_ready, 1)
                            if g == NG - 1:
                                dve.wait_ge(mean_psum, layer + 1)
                                dve.tensor_copy(mean[:, :], bank(1, 2)[:, 0:E1]).then_inc(mean_ready, 1)
                            continue
                        if g == DVE_AT[layer]:
                            epilogue(*before(pair, u))

                blocks(dve, bits)
                epilogue(NB // 2 - 1, 1)
                chain[0] += per * NB


def kernel(**inputs):
    import numpy as np
    import concourse.bacc as bacc
    from concourse import mybir as mb
    from concourse.bass_utils import run_bass_kernel_spmd

    a = {k: np.asarray(v) for k, v in inputs.items()}
    adj = a["adj"].reshape(P, NB, BT, P, NG, GT).transpose(1, 4, 3, 5, 2, 0).reshape(NB * NG, P, GT * BW)
    w = np.stack([a["L0_gnn_weight_w"], a["L1_gnn_W"][0], a["L1_gnn_W"][1]])
    arrays = {
        "x": a["x"],
        "adj": adj,
        "bias0": np.broadcast_to(a["L0_gnn_bias"], (P, C)),
        "mlp_b": np.broadcast_to(a["L1_gnn_mlp_b"], (P, C)),
        "w": w.transpose(1, 0, 2),
        "wT": w.transpose(2, 0, 1),
        "a0": a["L0_gnn_weight_a"].reshape(2, C)[::-1].T,
        "lT": a["L1_gnn_lin_w"].reshape(2, 2, C, HID).transpose(3, 0, 1, 2),
        "attn": a["L1_gnn_attn"][:, :, 0].T,
        "lin_b": a["L1_gnn_lin_b"].T,
        "mlp_w": a["L1_gnn_mlp_w"].reshape(LAYERS, C, C).transpose(1, 0, 2),
    }
    nc = bacc.Bacc("TRN2", target_bir_lowering=False, num_devices=1)
    sent, args = {}, []
    for name, value in arrays.items():
        value = np.ascontiguousarray(value)
        sent[f"{name}_dram"] = value
        args.append(nc.dram_tensor(f"{name}_dram", value.shape, mb.dt.from_np(value.dtype), kind="ExternalInput").ap())
    out = nc.dram_tensor("out_dram", (N, C), mb.dt.float32, kind="ExternalOutput").ap()
    build(nc, *args, out)
    r = run_bass_kernel_spmd(nc, [sent], core_ids=[0])
    return r.results[0]["out_dram"]
```

```python
from contextlib import ExitStack

import concourse.bass as bass
from concourse import mybir

F32 = mybir.dt.float32
BF16 = mybir.dt.bfloat16
FP8 = mybir.dt.float8e4
U8 = mybir.dt.uint8
I8 = mybir.dt.int8
U32 = mybir.dt.uint32
I32 = mybir.dt.int32
ALU = mybir.AluOpType
ACT = mybir.ActivationFunctionType
AX = mybir.AxisListType

P = 128
N = 4096
C = 64
E1 = C + 1
HID = 32
T = N // P
BT = 4
BW = BT * P
NB = T // BT
GT = 4
NG = T // GT
GW = GT * BW // 4
PARTS = 3
TSLOTS = 4
STAGES = 4
LAYERS = 3
ALPHA = (0.01, 0.2, 0.2)
SLOTS = (4, 8, 8)
SHIFT = 60.0
EPS = 1e-5
MIX = 0.2
BIT = (0x20, 0x10)
ACT_TILES = ((4,) * NG, (3,) * NG, (3,) * NG)
DVE_AT = (2, 6, 6)
PE_TURN_AT = (6, 4, 4)
PE_PROJ_AT = (7, 5, 5)
ACT_TURN_AT, ACT_PROJ_AT = 1, 2


def build(nc, x, adj, bias0, mlp_b, w, wT, a0, lT, attn, lin_b, mlp_w, out):
    x_v = x.rearrange("(p t) c -> p t c", t=T)
    out_v = out.rearrange("(p t) c -> p t c", t=T)

    with ExitStack() as ctx:
        def sb(name, shape, dt):
            return ctx.enter_context(nc.sbuf_tensor(name, shape, dt))

        def sem(name):
            return ctx.enter_context(nc.semaphore(name))

        mask = sb("mask", [P, NB // 2, NG * GW], U32)
        room = sb("room", [P, 8 * 2 * GW + STAGES * 4 * GW - 4 * 2 * GW], U32)
        signs = sb("signs", [P, TSLOTS, GW], U32)
        oddbits = sb("oddbits", [P, GW], U32)
        U = sb("U", [P, N], F32)
        Y = sb("Y", [P, T, 2 * PARTS * E1], BF16)
        Wh = sb("Wh", [P, T, E1], F32)
        X = sb("X", [P, T, C], F32)
        H = sb("H", [P, T, C], F32)
        yf = sb("yf", [P, 2, GT, 2, E1], F32)
        S = sb("S", [P, BT, 2, E1], F32)
        num = sb("num", [P, BT, E1], F32)
        num2 = sb("num2", [P, BT, E1], F32)
        hn = sb("hn", [P, 2, BT, C], F32)
        hT = sb("hT", [C, BW], F32)
        vu = sb("vu", [P, T, 2], F32)
        v = sb("v", [P, T], F32)
        nv = sb("nv", [P, T], F32)
        bd = sb("bd", [P, 2, T], F32)
        ac = sb("ac", [P, 2, T], F32)
        z = sb("z", [P, T], F32)
        az = sb("az", [P, T], F32)
        zm = sb("zm", [P, T], F32)
        vmax = sb("vmax", [P, 1], F32)
        vtop = sb("vtop", [1, 1], F32)
        V = sb("V", [P, 1], F32)
        whsum = sb("whsum", [P, E1], F32)
        mean = sb("mean", [P, E1], F32)
        small = sb("small", [P, 4, T], F32)
        half = sb("half", [P, T], F32)
        ident = sb("ident", [P, P], F32)
        ones = sb("ones", [P, P], F32)
        bias_sb = sb("bias_sb", [P, C], F32)
        mlpb_sb = sb("mlpb_sb", [P, C], F32)
        rhs = sb("rhs", [C, LAYERS, C + 2], F32)
        wub = sb("wub", [C, LAYERS, P], F32)
        avu = sb("avu", [C, LAYERS, 2], F32)
        attn_sb = sb("attn_sb", [HID, 2], F32)
        linb_sb = sb("linb_sb", [HID, 2], F32)
        mlp_sb = sb("mlp_sb", [C, LAYERS, C], F32)
        cc = sb("cc", [P, LAYERS], F32)
        ps = ctx.enter_context(nc.psum_tensor("ps", [P, 2, BT, 512], F32))

        params_in = sem("params_in")
        x_in = [sem("x_in0"), sem("x_in1")]
        adj_in = [sem(f"adj_in{s}") for s in range(STAGES)]
        stored = sem("stored")
        const_ready = sem("const_ready")
        cleared = sem("cleared")
        prep_psum = sem("prep_psum")
        prep_copied = sem("prep_copied")
        dve_step = sem("dve_step")
        var_ready = sem("var_ready")
        rstd_ready = sem("rstd_ready")
        centred = sem("centred")
        squared = sem("squared")
        stage_read = sem("stage_read")
        edges_ready = sem("edges_ready")
        act_signs = sem("act_signs")
        dve_signs = sem("dve_signs")
        neg_ready = sem("neg_ready")
        pos_ready = sem("pos_ready")
        bits_used = sem("bits_used")
        elu_in = sem("elu_in")
        elu_exp = sem("elu_exp")
        h_ready = sem("h_ready")
        turned = sem("turned")
        hT_ready = sem("hT_ready")
        projected = sem("projected")
        wh_ready = sem("wh_ready")
        x_added = sem("x_added")
        x_biased = sem("x_biased")
        part_max = sem("part_max")
        part_max_row = sem("part_max_row")
        top_ready = sem("top_ready")
        top_spread = sem("top_spread")
        exps_in = sem("exps_in")
        bd_ready = sem("bd_ready")
        ac_ready = sem("ac_ready")
        y_product = sem("y_product")
        y_high = sem("y_high")
        y_rest = sem("y_rest")
        y_mid = sem("y_mid")
        y_ready = sem("y_ready")
        whsum_ready = sem("whsum_ready")
        mean_psum = sem("mean_psum")
        mean_ready = sem("mean_ready")

        pe_passed = sem("pe_passed")
        act_passed = sem("act_passed")
        dve_passed = sem("dve_passed")

        def slot(s, which):
            return room[:, (2 * s + which) * GW:(2 * s + which + 1) * GW]

        def weights(s, which, j, i):
            at = (j * BT + i) * P
            return slot(s, which).bitcast(FP8)[:, at:at + P]

        def stage(q):
            at = 4 * 2 * GW + q * 4 * GW
            return room[:, at:at + 4 * GW].bitcast(I32)

        def edges(pair, g):
            return mask[:, bass.ds(pair, 1), g * GW:(g + 1) * GW].rearrange("p o w -> p (o w)")

        def urow(pair, u):
            return U[:, bass.ds((2 * pair + u) * BW, BW)]

        def tiles(t, pair, u):
            return t[:, bass.ds((2 * pair + u) * BT, BT)]

        def parts(g0, g1, part):
            return Y[:, g0:g1, :].rearrange("p t (g k c) -> p t g k c", g=2, k=PARTS)[:, :, :, part, :]

        prep = signs[:, :, :].rearrange("p s w -> p (s w)").bitcast(F32)
        wT_sb = prep[0:C, 0:LAYERS * C].rearrange("p (l c) -> p l c", l=LAYERS)
        lT_sb = prep[0:HID, 256:512].rearrange("p (l k c) -> p l k c", l=2, k=2)
        linb_w = prep[0:HID, 512:768].rearrange("p (l c) -> p l c", l=2)

        share = yf[:, :, :, :, :].rearrange("p s t k c -> p (s t k c)")[:, 0:2 * BT * C].rearrange(
            "p (s t c) -> p s t c", s=2, t=BT)

        def squares(t):
            return U[:, :].rearrange("p (t c) -> p t c", t=T)[:, t, 0:C]

        hT_first = Y[:, :, :].rearrange("p t c -> p (t c)").bitcast(F32)[0:C, 0:N].rearrange("p (b w) -> p b w", b=NB)

        def turned_h(layer, pair, u):
            return hT_first[:, 2 * pair + u, :] if layer < 0 else hT[:, :]

        def yhat(j, which):
            return Y[:, j, which * PARTS * E1:(which + 1) * PARTS * E1]

        def wide(ap, n):
            return ap.rearrange("p (t o) -> p t o", o=1).broadcast_to([P, ap.shape[1], n])

        def bank(u, b):
            return ps[:, u, b, :]

        def blocks(eng, body, peel_last=False):
            body(0, 0)
            body(0, 1)
            with eng.Fori(1, NB // 2 - peel_last) as pair:
                body(pair, 0)
                body(pair, 1)
            if peel_last:
                body(NB // 2 - 1, 0)
                body(NB // 2 - 1, 1)

        def before(pair, u):
            return (pair, 0) if u else (pair - 1, 1)

        def epi(layer, pair, u):
            return (2 * pair + u) + NB * (layer + 1)

        def shares(layer, pair, u):
            return (2 * pair + u) + (layer * NB + 3)

        def unit(layer, pair, u, g):
            return (2 * pair + u) * NG + g + layer * NB * NG

        block = ctx.enter_context(nc.Block())

        @block.sync
        def _(sp):
            sp.dma_start(X[:, 0:T // 2, :], x_v[:, 0:T // 2, :]).then_inc(x_in[0], 16)
            sp.dma_start(X[:, T // 2:T, :], x_v[:, T // 2:T, :]).then_inc(x_in[1], 16)
            sp.dma_start(rhs[:, :, 0:C], w).then_inc(params_in, 16)
            sp.dma_start(wT_sb[:, :, :], wT).then_inc(params_in, 16)
            sp.dma_start(avu[:, 0, :], a0).then_inc(params_in, 16)
            sp.dma_start(lT_sb[:, :, :, :], lT).then_inc(params_in, 16)
            sp.dma_start(attn_sb[:, :], attn).then_inc(params_in, 16)
            sp.dma_start(linb_sb[:, :], lin_b).then_inc(params_in, 16)
            sp.dma_start(mlp_sb[:, :, :], mlp_w).then_inc(params_in, 16)
            sp.dma_start(bias_sb[:, :], bias0).then_inc(params_in, 16)
            sp.dma_start(mlpb_sb[:, :], mlp_b).then_inc(params_in, 16)

            def load(pair, u):
                for g in range(NG):
                    G = (2 * pair + u) * NG + g
                    if not (isinstance(pair, int) and G < STAGES):
                        sp.wait_ge(stage_read, G - STAGES + 1)
                    sp.dma_start(stage(g % STAGES), adj[bass.ds(G, 1), :, :].rearrange("o p w -> (o p) w")
                                 ).then_inc(adj_in[g % STAGES], 16)

            blocks(sp, load)

            def store(pair, u):
                sp.wait_ge(x_added, shares(2, pair, u))
                sp.dma_start(out_v[:, bass.ds((2 * pair + u) * BT, BT), :], tiles(X, pair, u)).then_inc(stored, 16)

            blocks(sp, store)
            sp.wait_ge(stored, 16 * NB)

        @block.tensor
        def _(pe):
            pe.wait_ge(params_in, 16 * 9)
            pe.wait_ge(cleared, 4)
            for l in range(2):
                pe.matmul(bank(1, 3)[0:C, 2 * l:2 * l + 1], lT_sb[:, l, 1, :], attn_sb[:, l:l + 1], start=True, stop=True)
                pe.matmul(bank(1, 3)[0:C, 2 * l + 1:2 * l + 2], lT_sb[:, l, 0, :], attn_sb[:, l:l + 1], start=True, stop=True)
                last = pe.matmul(bank(1, 2)[:, l:l + 1], linb_w[:, l, :], attn_sb[:, l:l + 1], start=True, stop=True)
            last.then_inc(prep_psum, 1)
            pe.wait_ge(prep_copied, 1)
            for l in range(LAYERS):
                last = pe.matmul(bank(0, 2)[0:C, 2 * l:2 * l + 2], wT_sb[:, l, :], avu[:, l, :], start=True, stop=True)
            last.then_inc(prep_psum, 1)
            pe.wait_ge(const_ready, 1)

            def turn(layer, pair, u):
                e = epi(layer, pair, u)
                pe.wait_ge(h_ready, e + 1)
                if layer < 0 and pair >= 1:
                    pe.wait_ge(hT_ready, e - 1)
                pe.sem_inc(pe_passed, 1)
                for i in range(BT):
                    h = H[:, (2 * pair + u) * BT + i, :] if layer < 0 else hn[:, u, i, :]
                    last = pe.transpose(bank(u, 0)[0:C, i * P:(i + 1) * P], h, ident[:, :])
                last.then_inc(turned, 1)

            def project(layer, pair, u):
                e = epi(layer, pair, u)
                pe.wait_ge(hT_ready, e + 1)
                if layer < 0 and pair >= 1:
                    pe.wait_ge(wh_ready, e - 1)
                for i in range(BT):
                    h = turned_h(layer, pair, u)[:, i * P:(i + 1) * P]
                    if layer < 2:
                        last = pe.matmul(bank(u, 1)[:, i * (C + 2):(i + 1) * (C + 2)], h, rhs[:, layer + 1, :], start=True, stop=True)
                    if layer >= 0:
                        last = pe.matmul(bank(u, 2)[:, i * C:(i + 1) * C], h, mlp_sb[:, layer, :], start=True, stop=True)
                if layer < 2:
                    last = pe.matmul(bank(u, 3), wub[:, layer + 1, :], turned_h(layer, pair, u), start=True, stop=True)
                last.then_inc(projected, 1)

            for b in range(NB + 1):
                if b < NB:
                    turn(-1, b // 2, b % 2)
                if b == 0:
                    pe.wait_ge(prep_copied, 2)
                else:
                    project(-1, (b - 1) // 2, (b - 1) % 2)

            for layer in range(LAYERS):
                pe.wait_ge(part_max, layer + 1)
                pe.transpose(bank(1, 0)[0:1, 0:P], vmax[:, :], ident[:, :]).then_inc(part_max_row, 1)
                pe.wait_ge(top_ready, layer + 1)
                pe.matmul(bank(1, 1)[:, 0:1], ones[0:1, :], vtop[:, :], start=True, stop=True).then_inc(top_spread, 1)

                def sums(pair, u, layer=layer):
                    first = isinstance(pair, int) and pair == 0
                    if first and u:
                        pe.wait_ge(mean_ready, layer + 1)
                    if not first:
                        pe.wait_ge(wh_ready, epi(layer, pair, u) - 1)
                    for g in range(NG):
                        G = unit(layer, pair, u, g)
                        if g == PE_TURN_AT[layer] and not (first and not u):
                            turn(layer, *before(pair, u))
                        if g == PE_PROJ_AT[layer] and not (first and not u):
                            project(layer, *before(pair, u))
                        if first and not u:
                            if g == 4:
                                pe.wait_ge(whsum_ready, layer + 1)
                                pe.matmul(bank(1, 2)[:, 0:E1], ones[:, :], whsum[:, :], start=True, stop=True).then_inc(mean_psum, 1)
                            pe.wait_ge(y_ready, layer * NG + g + 1)
                        pe.wait_ge(pos_ready, G + 1)
                        pe.sem_inc(pe_passed, 1)
                        s = g % SLOTS[layer]
                        for jj in range(GT):
                            j = g * GT + jj
                            for i in range(BT):
                                for which in (1, 0):
                                    k = 1 - which
                                    last = pe.matmul(
                                        bank(u, i)[:, k * PARTS * E1:(k + 1) * PARTS * E1],
                                        weights(s, which, jj, i), yhat(j, k),
                                        start=(j == 0 and k == 0), stop=(j == T - 1), skip_group_check=True)
                        last.then_inc(bits_used, 1)

                blocks(pe, sums)
                turn(layer, NB // 2 - 1, 1)
                project(layer, NB // 2 - 1, 1)

        @block.gpsimd
        def _(pool):
            pool.memset(ident[:, :], 0.0).then_inc(cleared, 1)
            pool.memset(ones[:, :], 1.0).then_inc(cleared, 1)
            pool.memset(half[:, :], -0.5).then_inc(cleared, 1)
            pool.wait_ge(cleared, 3)
            pool.affine_select(out=ident[:, :], in_=ident[:, :], compare_op=ALU.not_equal, fill=1.0,
                               base=0, pattern=[[-1, P]], channel_multiplier=1).then_inc(const_ready, 1)

            def rstd(n, a, b):
                pool.wait_ge(var_ready, n + 1)
                pool.tensor_tensor(small[:, 2, a:b], small[:, 1, a:b], half[:, a:b], ALU.pow).then_inc(rstd_ready, 1)

            def all_tiles(t):
                return t[:, :].rearrange("p (o c) -> p o c", o=1).broadcast_to([P, T, C])

            rstd(0, 0, T // 2)
            rstd(1, T // 2, T)
            pool.wait_ge(params_in, 16 * 9)
            pool.tensor_tensor(X[:, :, :], X[:, :, :], all_tiles(bias_sb), ALU.add).then_inc(x_added, 2)

            for layer in range(LAYERS):
                for g in range(NG):
                    n = layer * NG + g
                    if g == 0:
                        pool.wait_ge(bd_ready, layer + 1)
                        pool.wait_ge(wh_ready, NB * (layer + 1))
                        if layer:
                            pool.wait_ge(x_added, shares(layer - 1, NB // 2 - 1, 1))
                    if n >= 2:
                        pool.wait_ge(y_ready, n - 1)
                    t = slice(g * GT, (g + 1) * GT)
                    for k in range(2):
                        last = pool.tensor_tensor(yf[:, g % 2, :, k, :], Wh[:, t, :], wide(bd[:, k, t], E1), ALU.mult)
                    last.then_inc(y_product, 1)

                def add(pair, u, layer=layer):
                    if layer == 0:
                        rstd(2 + (2 * pair + u), 0, BT)
                    pool.wait_ge(wh_ready, epi(layer, pair, u) + 1)
                    pool.tensor_tensor(tiles(X, pair, u), tiles(X, pair, u), share[:, u, :, :], ALU.add).then_inc(x_added, 1)

                if layer == 1:
                    pool.wait_ge(x_added, shares(0, NB // 2 - 1, 1))
                    pool.tensor_tensor(X[:, :, :], X[:, :, :], all_tiles(mlpb_sb), ALU.add).then_inc(x_biased, 1)
                    pool.wait_ge(x_biased, 1)
                blocks(pool, add)

        @block.scalar
        def _(act):
            def turn_out(layer, pair, u):
                e = epi(layer, pair, u)
                act.wait_ge(turned, e + 1)
                if layer >= 0:
                    act.wait_ge(projected, e)
                act.copy(turned_h(layer, pair, u), bank(u, 0)[0:C, :]).then_inc(hT_ready, 1)

            def project_out(layer, pair, u):
                act.wait_ge(projected, epi(layer, pair, u) + 1)
                if layer < 2:
                    both = bank(u, 1)[:, 0:BT * (C + 2)].rearrange("p (t c) -> p t c", t=BT)
                    act.copy(tiles(vu, pair, u), both[:, :, C:C + 2])
                    act.copy(tiles(Wh, pair, u)[:, :, 0:C], both[:, :, 0:C])
                    last = act.activation(urow(pair, u), bank(u, 3), ACT.Identity, bias=cc[:, layer + 1:layer + 2])
                if layer >= 0:
                    act.wait_ge(x_added, shares(layer, pair, u) - 2)
                    last = act.copy(share[:, u, :, :], bank(u, 2)[:, 0:BT * C].rearrange("p (t c) -> p t c", t=BT))
                last.then_inc(wh_ready, 1)

            act.wait_ge(centred, 1)
            for n in range(2):
                act.wait_ge(centred, n + 1)
                t = slice(n * T // 2, (n + 1) * T // 2)
                act.activation(squares(t), H[:, t, :], ACT.Square).then_inc(squared, 1)
            act.wait_ge(prep_copied, 1)
            for b in range(NB + 1):
                if b < NB:
                    turn_out(-1, b // 2, b % 2)
                if b:
                    project_out(-1, (b - 1) // 2, (b - 1) % 2)

            for layer in range(LAYERS):
                act.wait_ge(exps_in, 2 * layer + 1)
                act.activation(bd[:, :, :], bd[:, :, :], ACT.Exp).then_inc(bd_ready, 1)
                act.wait_ge(exps_in, 2 * layer + 2)
                act.activation(ac[:, :, :], ac[:, :, :], ACT.Exp).then_inc(ac_ready, 1)

                def signs_of(pair, u, layer=layer):
                    first = isinstance(pair, int) and pair == 0
                    for g in range(NG):
                        G = unit(layer, pair, u, g)
                        n = layer * NG + g
                        if first and not u:
                            act.wait_ge(y_product, n + 1)
                            act.copy(parts(g * GT, (g + 1) * GT, 0), yf[:, g % 2, :, :, :]).then_inc(y_high, 1)
                        if not (first and not u and g < TSLOTS and layer == 0):
                            act.wait_ge(neg_ready, G - TSLOTS + 1)
                        act.sem_inc(act_passed, 1)
                        s8 = signs[:, g % TSLOTS, :].bitcast(I8)
                        for jj in range(ACT_TILES[layer][g % 2]):
                            j = g * GT + jj
                            last = act.activation(s8[:, jj * BW:(jj + 1) * BW], urow(pair, u), ACT.Sign, bias=v[:, j:j + 1])
                        last.then_inc(act_signs, 1)
                        if first and not u:
                            act.wait_ge(y_rest, n + 1)
                            act.copy(parts(g * GT, (g + 1) * GT, 1), yf[:, g % 2, :, :, :]).then_inc(y_mid, 1)
                            continue
                        if layer and g == DVE_AT[layer]:
                            elu(*before(pair, u))
                        if g == ACT_TURN_AT and not first:
                            turn_out(layer, pair - 1, u)
                        if g == ACT_PROJ_AT and not first:
                            project_out(layer, pair - 1, u)

                def elu(pair, u, layer=layer):
                    act.wait_ge(elu_in, (2 * pair + u) + (layer - 1) * NB + 1)
                    act.activation(S[:, :, 0, 0:C], num2[:, :, 0:C], ACT.Exp).then_inc(elu_exp, 1)

                blocks(act, signs_of)
                turn_out(layer, NB // 2 - 1, 0)
                project_out(layer, NB // 2 - 1, 0)
                if layer:
                    elu(NB // 2 - 1, 1)
                turn_out(layer, NB // 2 - 1, 1)
                project_out(layer, NB // 2 - 1, 1)

        @block.vector
        def _(dve):
            chain = [0]

            def link(ins):
                chain[0] += 1
                ins.then_inc(dve_step, 1)
                dve.wait_ge(dve_step, chain[0])

            def steps(base, per, pair, u):
                at = [0]

                def step(ins):
                    at[0] += 1
                    assert at[0] <= per
                    ins.then_inc(dve_step, 1)
                    dve.wait_ge(dve_step, (2 * pair + u) * per + (base + at[0]))
                return step, at

            link(dve.memset(Wh[:, :, C:E1], 1.0))
            link(dve.memset(cc[:, 0:1], 0.0))

            halves = [slice(0, T // 2), slice(T // 2, T)]
            for n, t in enumerate(halves):
                dve.wait_ge(x_in[n], 16)
                link(dve.tensor_reduce(small[:, 0, t], X[:, t, :], AX.X, ALU.add))
                link(dve.tensor_scalar(small[:, 0, t], small[:, 0, t], 1.0 / C, None, ALU.mult))
                dve.tensor_tensor(H[:, t, :], X[:, t, :], wide(small[:, 0, t], C), ALU.subtract).then_inc(centred, 1)
            for n, t in enumerate(halves):
                dve.wait_ge(squared, n + 1)
                link(dve.tensor_reduce(small[:, 1, t], squares(t), AX.X, ALU.add))
                dve.tensor_scalar(small[:, 1, t], small[:, 1, t], 1.0 / C, EPS, ALU.mult, ALU.add).then_inc(var_ready, 1)
            dve.wait_ge(params_in, 16 * 9)
            dve.wait_ge(cleared, 3)
            for l in range(2):
                last = dve.tensor_scalar(linb_w[:, l, :], ones[0:HID, :], linb_sb[:, l:l + 1], None, ALU.mult)
            last.then_inc(cleared, 1)
            dve.wait_ge(prep_psum, 1)
            dve.tensor_copy(avu[:, 1:3, :], bank(1, 3)[0:C, 0:4].rearrange("p (l k) -> p l k", l=2))
            dve.tensor_copy(cc[:, 1:3], bank(1, 2)[:, 0:2]).then_inc(prep_copied, 1)

            for n, t in enumerate(halves):
                dve.wait_ge(rstd_ready, n + 1)
                link(dve.tensor_tensor(H[:, t, :], H[:, t, :], wide(small[:, 2, t], C), ALU.mult))
                dve.tensor_scalar(H[:, t, :], H[:, t, :], 0.0, None, ALU.max).then_inc(h_ready, NB // 2)
                if n == 0:
                    dve.wait_ge(prep_psum, 2)
                    link(dve.tensor_copy(rhs[:, :, C:C + 2], bank(0, 2)[0:C, 0:6].rearrange("p (l k) -> p l k", l=LAYERS)))
                    for l in range(LAYERS):
                        last = dve.tensor_scalar(wub[:, l, :], ones[0:C, :], rhs[:, l, C + 1:C + 2], None, ALU.mult)
                    last.then_inc(prep_copied, 1)

            def convert(pair, u, g):
                G = unit(0, pair, u, g)
                dve.wait_ge(adj_in[g % STAGES], (2 * pair + u) * 32 + 16 * (g // STAGES + 1))
                if u and not (isinstance(pair, int) and pair == 0 and g == 0):
                    dve.wait_ge(edges_ready, pair * NG + g)
                to = oddbits[:, :] if u else edges(pair, g)
                dve.tensor_scalar(to.bitcast(U8), stage(g % STAGES), 0.0, float(BIT[u]), ALU.is_gt, ALU.mult
                                  ).then_inc(stage_read, 1)
                if u:
                    dve.wait_ge(stage_read, G + 1)
                    dve.tensor_tensor(edges(pair, g), edges(pair, g), oddbits[:, :], ALU.bitwise_or).then_inc(edges_ready, 1)

            for u in range(2):
                for g in range(NG):
                    convert(0, u, g)

            signs_base = 0
            for layer in range(LAYERS):
                alpha = ALPHA[layer]
                dve.wait_ge(wh_ready, NB * (layer + 1))
                dve.reduce_max(vmax[:, :], vu[:, :, 0], AX.X).then_inc(part_max, 1)
                dve.tensor_copy(v[:, :], vu[:, :, 0])
                dve.tensor_scalar(nv[:, :], vu[:, :, 0], -1.0, None, ALU.mult)
                dve.wait_ge(part_max_row, layer + 1)
                dve.reduce_max(vtop[:, :], bank(1, 0)[0:1, 0:P], AX.X).then_inc(top_ready, 1)
                dve.wait_ge(top_spread, layer + 1)
                link(dve.tensor_copy(V[:, :], bank(1, 1)[:, 0:1]))
                dve.tensor_scalar(bd[:, 0, :], vu[:, :, 0], V[:, :], SHIFT, ALU.subtract, ALU.add)
                link(dve.tensor_scalar(bd[:, 1, :], vu[:, :, 0], V[:, :], alpha, ALU.subtract, ALU.mult))
                dve.tensor_scalar(bd[:, 1, :], bd[:, 1, :], SHIFT, None, ALU.add).then_inc(exps_in, 1)
                link(dve.tensor_scalar(z[:, :], vu[:, :, 1], cc[:, layer:layer + 1], V[:, :], ALU.add, ALU.add))
                link(dve.tensor_scalar(az[:, :], z[:, :], alpha, None, ALU.mult))
                link(dve.tensor_tensor(zm[:, :], z[:, :], az[:, :], ALU.max))
                dve.tensor_tensor(ac[:, 0, :], z[:, :], zm[:, :], ALU.subtract)
                dve.tensor_tensor(ac[:, 1, :], az[:, :], zm[:, :], ALU.subtract).then_inc(exps_in, 1)

                base = chain[0]
                per, per_sums = (15, 14) if layer == 0 else (9, 8)

                def rows(pair, u, layer=layer, base=base, per=per, per_sums=per_sums):
                    step, at = steps(base, per, pair, u)
                    dve.wait_ge(bits_used, unit(layer, pair, u, NG - 1) + 1)
                    dve.wait_ge(ac_ready, layer + 1)
                    dve.wait_ge(mean_ready, layer + 1)
                    for k in range(2):
                        last = dve.tensor_reduce(
                            S[:, :, k, :], ps[:, u, :, k * PARTS * E1:(k + 1) * PARTS * E1].rearrange("p t (q c) -> p t c q", q=PARTS),
                            AX.X, ALU.add)
                    step(last)
                    dve.tensor_tensor(num[:, :, :], S[:, :, 0, :], wide(tiles(ac[:, 0, :], pair, u), E1), ALU.mult)
                    step(dve.tensor_tensor(num2[:, :, :], S[:, :, 1, :], wide(tiles(ac[:, 1, :], pair, u), E1), ALU.mult))
                    step(dve.tensor_tensor(num[:, :, :], num[:, :, :], num2[:, :, :], ALU.add))
                    step(dve.tensor_scalar(small[:, 0, 0:BT], num[:, :, C], 0.0, None, ALU.is_equal))
                    step(dve.tensor_tensor(num2[:, :, :], mean[:, :].rearrange("p (o c) -> p o c", o=1).broadcast_to([P, BT, E1]),
                                           wide(small[:, 0, 0:BT], E1), ALU.mult))
                    step(dve.tensor_tensor(num[:, :, :], num[:, :, :], num2[:, :, :], ALU.add))
                    step(dve.reciprocal(small[:, 3, 0:BT], num[:, :, C]))
                    step(dve.tensor_tensor(num[:, :, 0:C], num[:, :, 0:C], wide(small[:, 3, 0:BT], C), ALU.mult))
                    if layer == 0:
                        dve.wait_ge(x_added, 2)
                        xt = tiles(X, pair, u)
                        step(dve.tensor_tensor(xt, xt, num[:, :, 0:C], ALU.add))
                        dve.sem_inc(dve_passed, 1)
                        step(dve.tensor_reduce(small[:, 0, 0:BT], xt, AX.X, ALU.add))
                        step(dve.tensor_scalar(small[:, 0, 0:BT], small[:, 0, 0:BT], 1.0 / C, None, ALU.mult))
                        step(dve.tensor_tensor(num[:, :, 0:C], xt, wide(small[:, 0, 0:BT], C), ALU.subtract))
                        step(dve.tensor_tensor(num2[:, :, 0:C], num[:, :, 0:C], num[:, :, 0:C], ALU.mult))
                        step(dve.tensor_reduce(small[:, 1, 0:BT], num2[:, :, 0:C], AX.X, ALU.add))
                        dve.tensor_scalar(small[:, 1, 0:BT], small[:, 1, 0:BT], 1.0 / C, EPS, ALU.mult, ALU.add).then_inc(var_ready, 1)
                    else:
                        dve.tensor_scalar(num2[:, :, 0:C], num[:, :, 0:C], 0.0, None, ALU.min).then_inc(elu_in, 1)
                    assert at[0] == per_sums

                def next_h(pair, u, layer=layer, base=base, per=per, per_sums=per_sums):
                    step, at = steps(base + per_sums, per, pair, u)
                    dve.wait_ge(turned, epi(layer, pair, u) - 1)
                    if layer == 0:
                        dve.wait_ge(rstd_ready, 2 + (2 * pair + u) + 1)
                        step(dve.tensor_tensor(num[:, :, 0:C], num[:, :, 0:C], wide(small[:, 2, 0:BT], C), ALU.mult))
                        dve.tensor_scalar(hn[:, u, :, :], num[:, :, 0:C], 0.0, None, ALU.max).then_inc(h_ready, 1)
                        dve.wait_ge(h_ready, epi(layer, pair, u) + 1)
                        dve.tensor_scalar(tiles(H, pair, u), hn[:, u, :, :], MIX, MIX - 1.0, ALU.mult, ALU.add)
                    else:
                        n = (2 * pair + u) + (layer - 1) * NB
                        dve.wait_ge(elu_exp, n + 1)
                        step(dve.scalar_tensor_tensor(out=num[:, :, 0:C], in0=num[:, :, 0:C], scalar=0.0, in1=S[:, :, 0, 0:C],
                                                      op0=ALU.max, op1=ALU.add))
                        dve.scalar_tensor_tensor(out=hn[:, u, :, :], in0=num[:, :, 0:C], scalar=1.0 - MIX,
                                                 in1=tiles(H, pair, u), op0=ALU.mult, op1=ALU.add).then_inc(h_ready, 1)
                    assert at[0] == per - per_sums

                own = [g for g in range(NG) if ACT_TILES[layer][g] < GT]

                def own_signs(pair, u, g, layer=layer, own=own, signs_base=signs_base):
                    if g not in own:
                        return
                    s8 = signs[:, g % TSLOTS, :].bitcast(U8)
                    for jj in range(ACT_TILES[layer][g], GT):
                        j = g * GT + jj
                        last = dve.tensor_scalar(s8[:, jj * BW:(jj + 1) * BW], urow(pair, u), nv[:, j:j + 1], float(BIT[0] | BIT[1]),
                                                 ALU.is_lt, ALU.mult)
                    last.then_inc(dve_signs, 1)

                def bits(pair, u, layer=layer, rows=rows, next_h=next_h, own_signs=own_signs, own=own, signs_base=signs_base):
                    first = isinstance(pair, int) and pair == 0
                    final = isinstance(pair, int) and pair == NB // 2 - 1
                    bit = BIT[u] * 0x01010101
                    if layer == 0:
                        dve.wait_ge(stage_read, unit(0, pair, u, NG - 1) + 1)
                        dve.wait_ge(edges_ready, (pair + 1) * NG)
                    own_signs(pair, u, 0)
                    for g in range(NG):
                        G = unit(layer, pair, u, g)
                        n = layer * NG + g
                        s = g % SLOTS[layer]
                        if first and not u:
                            dve.wait_ge(y_high, n + 1)
                            dve.tensor_tensor(yf[:, g % 2, :, :, :], yf[:, g % 2, :, :, :], parts(g * GT, (g + 1) * GT, 0),
                                              ALU.subtract).then_inc(y_rest, 1)
                        if g in own:
                            dve.wait_ge(dve_signs, (2 * pair + u) * len(own) + (signs_base + own.index(g) + 1))
                        dve.wait_ge(act_signs, G + 1)
                        if not (first and not u and g < SLOTS[layer]):
                            dve.wait_ge(bits_used, G - SLOTS[layer] + 1)
                        dve.scalar_tensor_tensor(out=slot(s, 0), in0=edges(pair, g), scalar=bit, in1=signs[:, g % TSLOTS, :],
                                                 op0=ALU.bitwise_and, op1=ALU.bitwise_and).then_inc(neg_ready, 1)
                        if g + 1 < NG:
                            own_signs(pair, u, g + 1)
                        if layer == 0 and not final:
                            convert(pair + 1, u, g)
                        dve.wait_ge(neg_ready, G + 1)
                        dve.scalar_tensor_tensor(out=slot(s, 1), in0=edges(pair, g), scalar=bit, in1=slot(s, 0),
                                                 op0=ALU.bitwise_and, op1=ALU.bitwise_xor).then_inc(pos_ready, 1)
                        if first and not u:
                            dve.wait_ge(y_mid, n + 1)
                            dve.tensor_tensor(parts(g * GT, (g + 1) * GT, 2), yf[:, g % 2, :, :, :], parts(g * GT, (g + 1) * GT, 1),
                                              ALU.subtract).then_inc(y_ready, 1)
                            if g == 1:
                                dve.tensor_reduce(whsum[:, :], Wh[:, :, :].rearrange("p t c -> p c t"), AX.X, ALU.add
                                                  ).then_inc(whsum_ready, 1)
                            if g == NG - 1:
                                dve.wait_ge(mean_psum, layer + 1)
                                dve.tensor_copy(mean[:, :], bank(1, 2)[:, 0:E1]).then_inc(mean_ready, 1)
                            continue
                        if g == DVE_AT[layer]:
                            rows(*before(pair, u))
                        if g == DVE_AT[layer] + 1:
                            next_h(*before(pair, u))

                blocks(dve, bits, peel_last=layer == 0)
                rows(NB // 2 - 1, 1)
                next_h(NB // 2 - 1, 1)
                chain[0] += per * NB
                signs_base += len(own) * NB


def kernel(**inputs):
    import numpy as np
    import concourse.bacc as bacc
    from concourse import mybir as mb
    from concourse.bass_utils import run_bass_kernel_spmd

    a = {k: np.asarray(v) for k, v in inputs.items()}
    adj = a["adj"].reshape(P, NB, BT, P, NG, GT).transpose(1, 4, 3, 5, 2, 0).reshape(NB * NG, P, GT * BW)
    w = np.stack([a["L0_gnn_weight_w"], a["L1_gnn_W"][0], a["L1_gnn_W"][1]])
    arrays = {
        "x": a["x"],
        "adj": adj,
        "bias0": np.broadcast_to(a["L0_gnn_bias"], (P, C)),
        "mlp_b": np.broadcast_to(a["L1_gnn_mlp_b"], (P, C)),
        "w": w.transpose(1, 0, 2),
        "wT": w.transpose(2, 0, 1),
        "a0": a["L0_gnn_weight_a"].reshape(2, C)[::-1].T,
        "lT": a["L1_gnn_lin_w"].reshape(2, 2, C, HID).transpose(3, 0, 1, 2),
        "attn": a["L1_gnn_attn"][:, :, 0].T,
        "lin_b": a["L1_gnn_lin_b"].T,
        "mlp_w": a["L1_gnn_mlp_w"].reshape(LAYERS, C, C).transpose(1, 0, 2),
    }
    nc = bacc.Bacc("TRN2", target_bir_lowering=False, num_devices=1)
    sent, args = {}, []
    for name, value in arrays.items():
        value = np.ascontiguousarray(value)
        sent[f"{name}_dram"] = value
        args.append(nc.dram_tensor(f"{name}_dram", value.shape, mb.dt.from_np(value.dtype), kind="ExternalInput").ap())
    out = nc.dram_tensor("out_dram", (N, C), mb.dt.float32, kind="ExternalOutput").ap()
    build(nc, *args, out)
    r = run_bass_kernel_spmd(nc, [sent], core_ids=[0])
    return r.results[0]["out_dram"]
```

```python
from contextlib import ExitStack

import concourse.bass as bass
from concourse import mybir

F32 = mybir.dt.float32
BF16 = mybir.dt.bfloat16
FP8 = mybir.dt.float8e4
U8 = mybir.dt.uint8
I8 = mybir.dt.int8
U32 = mybir.dt.uint32
I32 = mybir.dt.int32
ALU = mybir.AluOpType
ACT = mybir.ActivationFunctionType
AX = mybir.AxisListType

P = 128
N = 4096
C = 64
E1 = C + 1
HID = 32
RW = 2 * C + 2
T = N // P
BT = 4
BW = BT * P
NB = T // BT
GT = 4
NG = T // GT
GW = GT * BW // 4
PARTS = 3
TSLOTS = 4
STAGES = 4
LAYERS = 3
ROW_STEPS = (11, 9, 9)
QUARTERS = 4
ALPHA = (0.01, 0.2, 0.2)
SLOTS = (4, 8, 8)
SHIFT = 60.0
EPS = 1e-5
MIX = 0.2
BIT = (0x20, 0x10)
FIRST_TILES = (3, 2, 2)
ACT_TILES = (4, 3, 3)
SPREAD_FROM, NEXT_H_AT = 3 * 2 + 0, 3 * 6 + 1
PE_TURN_AT, PE_PROJ_AT = 6, 7
ELU_AT = 6
POOL_STEPS = (4, 8, 11)
POOL_AT = (3, 4, 5)
TAKE_AT = 7
PE_LAST = (0, 1, 5, 6)
ACT_TURN_AT, ACT_PROJ_AT, ACT_FETCH_AT = 1, 3, 5


def build(nc, x, adj, bias0, mlp_b, w, wT, a0, lT, attn, lin_b, mlp_w, u_rows, out):
    x_v = x.rearrange("(p t) c -> p t c", t=T)
    out_v = out.rearrange("(p t) c -> p t c", t=T)

    with ExitStack() as ctx:
        def sb(name, shape, dt):
            return ctx.enter_context(nc.sbuf_tensor(name, shape, dt))

        def sem(name):
            return ctx.enter_context(nc.semaphore(name))

        mask = sb("mask", [P, NB // 2, NG * GW], U32)
        room = sb("room", [P, 8 * 2 * GW + STAGES * 4 * GW - 4 * 2 * GW], U32)
        signs = sb("signs", [P, TSLOTS, GW], U32)
        oddbits = sb("oddbits", [P, 2, GW], U32)
        U = sb("U", [P, N], F32)
        Y = sb("Y", [P, T, 2 * PARTS * E1], BF16)
        Wh = sb("Wh", [P, T, E1], F32)
        X = sb("X", [P, T, C], F32)
        H = sb("H", [P, T, C], F32)
        yf = sb("yf", [P, 2, GT, 2, E1], F32)
        S = sb("S", [P, BT, 2, E1], F32)
        num = sb("num", [P, BT, E1], F32)
        num2 = sb("num2", [P, BT, E1], F32)
        hn = sb("hn", [P, 2, BT, C], F32)
        hT = sb("hT", [C, BW], F32)
        vu = sb("vu", [P, T, 2], F32)
        vc = sb("vc", [P, T], F32)
        nvc = sb("nvc", [P, T], F32)
        bd = sb("bd", [P, 2, T], F32)
        ac = sb("ac", [P, 2, T], F32)
        z = sb("z", [P, T], F32)
        az = sb("az", [P, T], F32)
        zm = sb("zm", [P, T], F32)
        vmax = sb("vmax", [P, 1], F32)
        vtop = sb("vtop", [1, 1], F32)
        V = sb("V", [P, 1], F32)
        whsum = sb("whsum", [P, BT, E1], F32)
        stats = sb("stats", [P, BT, 6], F32)
        mv = sb("mv", [P, BT, 2], F32)
        mean = sb("mean", [P, E1], F32)
        small = sb("small", [P, 4, T], F32)
        minus_half = sb("minus_half", [P, T], F32)
        offset = sb("offset", [P, BT], F32)
        ident = sb("ident", [P, P], F32)
        ones = sb("ones", [P, P], F32)
        bias_sb = sb("bias_sb", [P, C], F32)
        mlpb_sb = sb("mlpb_sb", [P, C], F32)
        rhs = sb("rhs", [C, LAYERS, RW], F32)
        avu = sb("avu", [C, LAYERS, 2], F32)
        attn_sb = sb("attn_sb", [HID, 2], F32)
        linb_sb = sb("linb_sb", [HID, 2], F32)
        cc = sb("cc", [P, LAYERS], F32)
        ps = ctx.enter_context(nc.psum_tensor("ps", [P, 2, BT, 512], F32))

        params_in = sem("params_in")
        x_in = [sem(f"x_in{n}") for n in range(QUARTERS)]
        adj_in = [sem(f"adj_in{s}") for s in range(STAGES)]
        stored = sem("stored")
        const_ready = sem("const_ready")
        cleared = sem("cleared")
        offset_ready = sem("offset_ready")
        prep_psum = sem("prep_psum")
        prep_copied = sem("prep_copied")
        dve_step = sem("dve_step")
        row_step = sem("row_step")
        var_ready = sem("var_ready")
        var_raised = sem("var_raised")
        rstd_ready = sem("rstd_ready")
        centred = sem("centred")
        squared = sem("squared")
        stage_read = sem("stage_read")
        edges_ready = sem("edges_ready")
        act_signs = sem("act_signs")
        dve_signs = sem("dve_signs")
        neg_ready = sem("neg_ready")
        pos_ready = sem("pos_ready")
        bits_used = sem("bits_used")
        half_used = sem("half_used")
        elu_in = sem("elu_in")
        elu_exp = sem("elu_exp")
        h_ready = sem("h_ready")
        turned = sem("turned")
        hT_ready = sem("hT_ready")
        projected = sem("projected")
        vu_ready = sem("vu_ready")
        wh_ready = sem("wh_ready")
        share_ready = sem("share_ready")
        u_stored = [sem("u_stored0"), sem("u_stored1")]
        u_in = [sem("u_in0"), sem("u_in1")]
        u_first_stored = sem("u_first_stored")
        u_rest_stored = sem("u_rest_stored")
        u_first_in = sem("u_first_in")
        u_rest_in = sem("u_rest_in")
        x_added = sem("x_added")
        x_biased = sem("x_biased")
        part_max = sem("part_max")
        part_max_row = sem("part_max_row")
        top_ready = sem("top_ready")
        top_spread = sem("top_spread")
        vc_ready = sem("vc_ready")
        exps_in = sem("exps_in")
        bd_ready = sem("bd_ready")
        ac_ready = sem("ac_ready")
        y_product = sem("y_product")
        y_high = sem("y_high")
        y_rest = sem("y_rest")
        y_mid = sem("y_mid")
        y_ready = sem("y_ready")
        wh_summed = sem("wh_summed")
        sum_cleared = sem("sum_cleared")
        h_kept = sem("h_kept")
        h_scaled = sem("h_scaled")
        mean_psum = sem("mean_psum")
        mean_ready = sem("mean_ready")

        pe_passed = sem("pe_passed")
        act_passed = sem("act_passed")
        dve_passed = sem("dve_passed")
        pool_passed = sem("pool_passed")

        def quarter(n):
            return slice(n * T // QUARTERS, (n + 1) * T // QUARTERS)

        def slot(s, which):
            return room[:, (2 * s + which) * GW:(2 * s + which + 1) * GW]

        def weights(s, which, j, i):
            at = (j * BT + i) * P
            return slot(s, which).bitcast(FP8)[:, at:at + P]

        def stage(q):
            at = 4 * 2 * GW + q * 4 * GW
            return room[:, at:at + 4 * GW].bitcast(I32)

        def edges(pair, g):
            return mask[:, bass.ds(pair, 1), g * GW:(g + 1) * GW].rearrange("p o w -> p (o w)")

        def urow(pair, u):
            return U[:, bass.ds((2 * pair + u) * BW, BW)]

        def tiles(t, pair, u):
            return t[:, bass.ds((2 * pair + u) * BT, BT)]

        def parts(g0, g1, part):
            return Y[:, g0:g1, :].rearrange("p t (g k c) -> p t g k c", g=2, k=PARTS)[:, :, :, part, :]

        prep = signs[:, :, :].rearrange("p s w -> p (s w)").bitcast(F32)
        wT_sb = prep[0:C, 0:LAYERS * C].rearrange("p (l c) -> p l c", l=LAYERS)
        lT_sb = prep[0:HID, 256:512].rearrange("p (l k c) -> p l k c", l=2, k=2)
        linb_w = prep[0:HID, 512:768].rearrange("p (l c) -> p l c", l=2)

        share = yf[:, :, :, :, :].rearrange("p s t k c -> p (s t k c)")[:, 0:2 * BT * C].rearrange(
            "p (s t c) -> p s t c", s=2, t=BT)

        def squares(t):
            return U[:, :].rearrange("p (t c) -> p t c", t=T)[:, t, 0:C]

        hT_first = Y[:, :, :].rearrange("p t c -> p (t c)").bitcast(F32)[0:C, 0:N].rearrange("p (b w) -> p b w", b=NB)

        def turned_h(layer, pair, u):
            return hT_first[:, 2 * pair + u, :] if layer < 0 else hT[:, :]

        def yhat(j, which):
            return Y[:, j, which * PARTS * E1:(which + 1) * PARTS * E1]

        def wide(ap, n):
            return ap.rearrange("p (t o) -> p t o", o=1).broadcast_to([P, ap.shape[1], n])

        def bank(u, b):
            return ps[:, u, b, :]

        def blocks(eng, body, peel_last=False):
            body(0, 0)
            body(0, 1)
            with eng.Fori(1, NB // 2 - peel_last) as pair:
                body(pair, 0)
                body(pair, 1)
            if peel_last:
                body(NB // 2 - 1, 0)
                body(NB // 2 - 1, 1)

        def slot_of(layer, pair, u, g):
            return g if is_last(pair, u) else g % SLOTS[layer]

        def before(pair, u):
            return (pair, 0) if u else (pair - 1, 1)

        def urow_count(layer, pair):
            return (pair + (NB // 2) * layer) * 16 + 16

        LAST = (NB // 2 - 1, 1)

        def is_last(pair, u):
            return isinstance(pair, int) and (pair, u) == LAST

        def tt(half):
            return slice(0, BT) if half is None else slice(half * BT // 2, (half + 1) * BT // 2)

        def buf(u, half):
            return u if half is None else half

        def nth(pair, u, half=None):
            return 2 * pair + (u + 1 if half == 1 else u)

        def back(half):
            return 1 if half == 0 else 2

        def epi(layer, pair, u, half=None):
            return nth(pair, u, half) + ((NB + 1) * layer + NB)

        def share_no(layer, pair, u, half=None):
            return nth(pair, u, half) + (NB + 1) * layer

        def shares(layer, pair, u, half=None):
            return nth(pair, u, half) + ((NB + 1) * layer + 3)

        def inputs_epi(pair, u):
            return 2 * pair + u

        def unit(layer, pair, u, g):
            return (2 * pair + u) * NG + g + layer * NB * NG

        block = ctx.enter_context(nc.Block())

        @block.sync
        def _(sp):
            for n in range(QUARTERS):
                sp.dma_start(X[:, quarter(n), :], x_v[:, quarter(n), :]).then_inc(x_in[n], 16)
            sp.dma_start(rhs[:, :, 0:C], w).then_inc(params_in, 16)
            sp.dma_start(wT_sb[:, :, :], wT).then_inc(params_in, 16)
            sp.dma_start(avu[:, 0, :], a0).then_inc(params_in, 16)
            sp.dma_start(lT_sb[:, :, :, :], lT).then_inc(params_in, 16)
            sp.dma_start(attn_sb[:, :], attn).then_inc(params_in, 16)
            sp.dma_start(linb_sb[:, :], lin_b).then_inc(params_in, 16)
            sp.dma_start(rhs[:, :, C + 2:RW], mlp_w).then_inc(params_in, 16)
            sp.dma_start(bias_sb[:, :], bias0).then_inc(params_in, 16)
            sp.dma_start(mlpb_sb[:, :], mlp_b).then_inc(params_in, 16)

            def load(pair, u):
                for g in range(NG):
                    G = (2 * pair + u) * NG + g
                    if not (isinstance(pair, int) and G < STAGES):
                        sp.wait_ge(stage_read, G - STAGES + 1)
                    sp.dma_start(stage(g % STAGES), adj[bass.ds(G, 1), :, :].rearrange("o p w -> (o p) w")
                                 ).then_inc(adj_in[g % STAGES], 16)

            blocks(sp, load)

            def store(pair, u):
                for half in (0, 1) if is_last(pair, u) else (None,):
                    sp.wait_ge(x_added, shares(2, pair, u, half))
                    sp.dma_start(tiles(out_v, pair, u)[:, tt(half), :], tiles(X, pair, u)[:, tt(half), :]).then_inc(stored, 16)

            blocks(sp, store, peel_last=True)
            sp.wait_ge(stored, 16 * (NB + 1))

        @block.tensor
        def _(pe):
            pe.wait_ge(params_in, 16 * 9)
            pe.wait_ge(cleared, 4)
            for l in range(2):
                pe.matmul(bank(1, 3)[0:C, 2 * l:2 * l + 1], lT_sb[:, l, 1, :], attn_sb[:, l:l + 1], start=True, stop=True)
                pe.matmul(bank(1, 3)[0:C, 2 * l + 1:2 * l + 2], lT_sb[:, l, 0, :], attn_sb[:, l:l + 1], start=True, stop=True)
                last = pe.matmul(bank(1, 2)[:, l:l + 1], linb_w[:, l, :], attn_sb[:, l:l + 1], start=True, stop=True)
            last.then_inc(prep_psum, 1)
            pe.wait_ge(prep_copied, 1)
            for l in range(LAYERS):
                last = pe.matmul(bank(0, 3)[0:C, 2 * l:2 * l + 2], wT_sb[:, l, :], avu[:, l, :], start=True, stop=True)
            last.then_inc(prep_psum, 1)
            pe.wait_ge(const_ready, 1)

            def turn(layer, pair, u, half=None):
                e = inputs_epi(pair, u) if layer < 0 else epi(layer, pair, u, half)
                k = buf(u, half)
                pe.wait_ge(h_ready, e + 1)
                if layer < 0 and pair >= 1:
                    pe.wait_ge(hT_ready, e - 1)
                if half == 0:
                    pe.wait_ge(share_ready, share_no(layer, pair, u, half))
                pe.sem_inc(pe_passed, 1)
                for i in range(BT)[tt(half)]:
                    h = H[:, (2 * pair + u) * BT + i, :] if layer < 0 else hn[:, k, i, :]
                    last = pe.transpose(bank(k, 0)[0:C, i * P:(i + 1) * P], h, ident[:, :])
                last.then_inc(turned, 1)

            def project(layer, pair, u, half=None):
                e = inputs_epi(pair, u) if layer < 0 else epi(layer, pair, u, half)
                k = buf(u, half)
                pe.wait_ge(hT_ready, e + 1)
                if layer < 0 and pair >= 1:
                    pe.wait_ge(wh_ready, e - 1)
                cols = slice(0, C + 2) if layer < 0 else slice(0, RW) if layer < 2 else slice(C + 2, RW)
                for i in range(BT)[tt(half)]:
                    at = i % 2 * RW
                    last = pe.matmul(bank(k, 1 + i // 2)[:, at + cols.start:at + cols.stop], turned_h(layer, pair, u)[:, i * P:(i + 1) * P],
                                     rhs[:, (layer + 1) % LAYERS, cols], start=True, stop=True)
                last.then_inc(projected, 1)

            for b in range(NB + 1):
                if b < NB:
                    turn(-1, b // 2, b % 2)
                if b == 0:
                    pe.wait_ge(prep_copied, 2)
                else:
                    project(-1, (b - 1) // 2, (b - 1) % 2)

            for layer in range(LAYERS):
                pe.wait_ge(part_max, layer + 1)
                pe.transpose(bank(1, 0)[0:1, 0:P], vmax[:, :], ident[:, :]).then_inc(part_max_row, 1)
                pe.wait_ge(top_ready, layer + 1)
                pe.matmul(bank(1, 1)[:, 0:1], ones[0:1, :], vtop[:, :], start=True, stop=True).then_inc(top_spread, 1)

                def sums(pair, u, layer=layer):
                    first = isinstance(pair, int) and pair == 0
                    if first and u:
                        pe.wait_ge(mean_ready, layer + 1)
                    if not first:
                        pe.wait_ge(share_ready, share_no(layer, pair, u) - 1)

                    def products(g, which_i):
                        s = slot_of(layer, pair, u, g)
                        for jj in range(GT):
                            j = g * GT + jj
                            for i in which_i:
                                for which in (1, 0):
                                    k = 1 - which
                                    last = pe.matmul(
                                        bank(u, i)[:, k * PARTS * E1:(k + 1) * PARTS * E1],
                                        weights(s, which, jj, i), yhat(j, k),
                                        start=(j == 0 and k == 0), stop=(j == T - 1), skip_group_check=True)
                        return last

                    if is_last(pair, u):
                        for g in range(NG):
                            pe.wait_ge(pos_ready, unit(layer, pair, u, g) + 1)
                            last = products(g, range(BT)[tt(0)])
                        last.then_inc(half_used, 1)
                        for g in range(NG):
                            if g == PE_LAST[0]:
                                turn(layer, *before(pair, u))
                            if g == PE_LAST[1]:
                                project(layer, *before(pair, u))
                            if g == PE_LAST[2]:
                                turn(layer, pair, u, 0)
                            if g == PE_LAST[3]:
                                project(layer, pair, u, 0)
                            products(g, range(BT)[tt(1)]).then_inc(bits_used, 1)
                        return

                    for g in range(NG):
                        G = unit(layer, pair, u, g)
                        if g == PE_TURN_AT and not (first and not u):
                            turn(layer, *before(pair, u))
                        if g == PE_PROJ_AT and not (first and not u):
                            project(layer, *before(pair, u))
                        if first and not u:
                            if g == 4:
                                pe.wait_ge(wh_summed, epi(layer, 0, 0))
                                for i in range(BT):
                                    last = pe.matmul(bank(1, 2)[:, 0:E1], ones[:, :], whsum[:, i, :], start=(i == 0), stop=(i == BT - 1))
                                last.then_inc(mean_psum, 1)
                            pe.wait_ge(y_ready, layer * NG + g + 1)
                        pe.wait_ge(pos_ready, G + 1)
                        pe.sem_inc(pe_passed, 1)
                        products(g, range(BT)).then_inc(bits_used, 1)

                blocks(pe, sums, peel_last=True)
                turn(layer, *LAST, 1)
                project(layer, *LAST, 1)

        @block.gpsimd
        def _(pool):
            pool.memset(ident[:, :], 0.0).then_inc(cleared, 1)
            pool.memset(ones[:, :], 1.0).then_inc(cleared, 1)
            pool.memset(minus_half[:, :], -0.5).then_inc(cleared, 1)
            pool.memset(offset[:, :], MIX - 1.0).then_inc(offset_ready, 1)
            pool.wait_ge(offset_ready, 1)
            pool.wait_ge(cleared, 3)
            pool.affine_select(out=ident[:, :], in_=ident[:, :], compare_op=ALU.not_equal, fill=1.0,
                               base=0, pattern=[[-1, P]], channel_multiplier=1).then_inc(const_ready, 1)

            def rstd(n, to, var):
                pool.wait_ge(var_ready, n + 1)
                pool.sem_inc(pool_passed, 1)
                pool.tensor_scalar(to, var, EPS, None, ALU.add).then_inc(var_raised, 1)
                pool.wait_ge(var_raised, n + 1)
                pool.tensor_tensor(to, to, minus_half[:, 0:to.shape[1]], ALU.pow).then_inc(rstd_ready, 1)

            def sum_wh(layer, pair, u, half=None):
                e = epi(layer - 1, pair, u, half) if layer else inputs_epi(pair, u)
                to = whsum[:, tt(half), :]
                pool.wait_ge(wh_ready, e + 1)
                if not (layer == 0 and (pair, u) == (0, 0)):
                    pool.wait_ge(wh_summed, e)
                pool.tensor_tensor(to, to, tiles(Wh, pair, u)[:, tt(half), :], ALU.add).then_inc(wh_summed, 1)

            def clear_sum(n):
                pool.memset(whsum[:, :, :], 0.0).then_inc(sum_cleared, 1)
                pool.wait_ge(sum_cleared, n + 1)

            def all_tiles(t):
                return t[:, :].rearrange("p (o c) -> p o c", o=1).broadcast_to([P, T, C])

            for n in range(QUARTERS):
                t = quarter(n)
                rstd(n, small[:, 2, t], small[:, 1, t])
            pool.wait_ge(params_in, 16 * 9)
            pool.tensor_tensor(X[:, :, :], X[:, :, :], all_tiles(bias_sb), ALU.add).then_inc(x_added, 2)

            clear_sum(0)
            for b in range(NB):
                sum_wh(0, b // 2, b % 2)

            for layer in range(LAYERS):
                def product(g, layer=layer):
                    n = layer * NG + g
                    if n >= 2:
                        pool.wait_ge(y_ready, n - 1)
                    t = slice(g * GT, (g + 1) * GT)
                    for k in range(2):
                        last = pool.tensor_tensor(yf[:, g % 2, :, k, :], Wh[:, t, :], wide(bd[:, k, t], E1), ALU.mult)
                    last.then_inc(y_product, 1)

                def join(pair, g):
                    pool.wait_ge(stage_read, unit(0, pair, 1, g) + 1)
                    pool.wait_ge(pos_ready, unit(0, pair, 0, g) + 1)
                    pool.tensor_tensor(edges(pair, g), edges(pair, g), oddbits[:, g % 2, :], ALU.add).then_inc(edges_ready, 1)

                pool.wait_ge(bd_ready, layer + 1)
                if layer:
                    pool.wait_ge(x_added, shares(layer - 1, *LAST, 1))
                product(0)
                product(1)
                for g in range(NG):
                    pool.wait_ge(y_mid, layer * NG + g + 1)
                    pool.tensor_tensor(parts(g * GT, (g + 1) * GT, 2), yf[:, g % 2, :, :, :], parts(g * GT, (g + 1) * GT, 1),
                                       ALU.subtract).then_inc(y_ready, 1)
                    if g + 2 < NG:
                        product(g + 2)
                    if layer == 0:
                        join(0, g)

                if layer < 2:
                    pool.wait_ge(mean_psum, layer + 1)
                    clear_sum(layer + 1)

                def add(pair, u, layer=layer):
                    first = isinstance(pair, int) and pair == 0
                    for g in range(NG):
                        if g == TAKE_AT and not first:
                            take(pair - 1, u)
                        if layer == 0 and g in POOL_AT and not (first and not u):
                            row_step_of_pool(POOL_STEPS[POOL_AT.index(g)], *before(pair, u))
                        if layer == 0 and not u and not first:
                            join(pair, g)
                    if layer == 0 and not (first and not u):
                        keep(*before(pair, u))

                def row_step_of_pool(s, pair, u):
                    n = 2 * pair + u
                    if s == 4:
                        pool.wait_ge(mean_ready, 1)
                        pool.wait_ge(row_step, n * ROW_STEPS[0] + s)
                        pool.sem_inc(pool_passed, 1)
                        last = pool.tensor_tensor(S[:, :, 0, :], mean[:, :].rearrange("p (o c) -> p o c", o=1).broadcast_to([P, BT, E1]),
                                                  wide(small[:, 0, 0:BT], E1), ALU.mult)
                    elif s == 8:
                        pool.wait_ge(x_added, 2)
                        pool.wait_ge(row_step, n * ROW_STEPS[0] + s)
                        pool.sem_inc(pool_passed, 1)
                        last = pool.tensor_tensor(tiles(X, pair, u), tiles(X, pair, u), num[:, :, 0:C], ALU.add)
                    else:
                        factor(pair, u)
                        last = pool.tensor_tensor(num[:, :, 0:C], tiles(X, pair, u), wide(mv[:, :, 0], C), ALU.subtract)
                    last.then_inc(row_step, 1)

                def factor(pair, u, half=None):
                    rstd(QUARTERS + nth(pair, u, half), small[:, 2, tt(half)], mv[:, tt(half), 1])

                def keep(pair, u, half=None):
                    t = tt(half)
                    n = nth(pair, u, half)
                    pool.wait_ge(h_ready, epi(0, pair, u, half) + 1)
                    pool.sem_inc(pool_passed, 1)
                    pool.tensor_scalar(num2[:, t, 0:C], hn[:, buf(u, half), t, :], 0.0, MIX, ALU.max, ALU.mult).then_inc(h_scaled, 1)
                    pool.wait_ge(h_scaled, n + 1)
                    pool.tensor_tensor(tiles(H, pair, u)[:, t, :], num2[:, t, 0:C], wide(offset[:, t], C), ALU.add).then_inc(h_kept, 1)

                def take(pair, u, half=None, layer=layer):
                    if layer < 2:
                        sum_wh(layer + 1, pair, u, half)
                    pool.wait_ge(share_ready, share_no(layer, pair, u, half) + 1)
                    pool.sem_inc(pool_passed, 1)
                    xt = tiles(X, pair, u)[:, tt(half), :]
                    pool.tensor_tensor(xt, xt, share[:, buf(u, half), tt(half), :], ALU.add).then_inc(x_added, 1)

                if layer == 1:
                    pool.wait_ge(x_added, shares(0, *LAST, 1))
                    pool.tensor_tensor(X[:, :, :], X[:, :, :], all_tiles(mlpb_sb), ALU.add).then_inc(x_biased, 1)
                    pool.wait_ge(x_biased, 1)
                blocks(pool, add)
                take(*before(*LAST))
                for half in range(2):
                    if layer == 0:
                        factor(*LAST, half)
                        keep(*LAST, half)
                    take(*LAST, half)

        @block.scalar
        def _(act):
            def turn_out(layer, pair, u, half=None):
                e = inputs_epi(pair, u) if layer < 0 else epi(layer, pair, u, half)
                cols = slice(0, BW) if half is None else slice(half * BW // 2, (half + 1) * BW // 2)
                act.wait_ge(turned, e + 1)
                if layer >= 0 and not (isinstance(pair, int) and e == NB):
                    act.wait_ge(projected, e)
                act.sem_inc(act_passed, 1)
                act.activation(turned_h(layer, pair, u)[:, cols], bank(buf(u, half), 0)[0:C, cols],
                               ACT.Relu if layer <= 0 else ACT.Copy).then_inc(hT_ready, 1)

            def project_out(layer, pair, u, half=None):
                e = inputs_epi(pair, u) if layer < 0 else epi(layer, pair, u, half)
                k = buf(u, half)
                act.wait_ge(projected, e + 1)
                rows2 = slice(0, 2) if half is None else slice(half, half + 1)
                made = ps[:, k, 1:3, 0:2 * RW].rearrange("p b (i c) -> p b i c", i=2)[:, rows2]

                def by_two(ap):
                    return ap.rearrange("p (b i) c -> p b i c", i=2)[:, rows2]

                if layer < 2:
                    act.copy(by_two(tiles(vu, pair, u)), made[:, :, :, C:C + 2]).then_inc(vu_ready, 1)
                    act.copy(by_two(tiles(Wh, pair, u))[:, :, :, 0:C], made[:, :, :, 0:C]).then_inc(wh_ready, 1)
                if 0 <= layer < 2 and half != 0:
                    act.wait_ge(vu_ready, e + 1)
                    act.dma_start(u_rows[bass.ds(2 * pair + u, 1), :, :].rearrange("o t p -> p (o t)"),
                                  tiles(vu, pair, u)[:, :, 1], allow_slow_non_contiguous=True).then_inc(u_stored[u], 16)
                if layer >= 0:
                    act.wait_ge(x_added, shares(layer, pair, u, half) - back(half))
                    act.copy(by_two(share[:, k, :, :]), made[:, :, :, C + 2:RW]).then_inc(share_ready, 1)

            def fetch(layer, pair, u):
                act.wait_ge(u_stored[u], urow_count(layer, pair))
                act.dma_start(urow(pair, u), u_rows[bass.ds(2 * pair + u, 1), :, :].rearrange("o t p -> o (t p)").broadcast_to([P, BW])
                              ).then_inc(u_in[u], 16)

            u_line = u_rows.rearrange("b t p -> (b t p)").rearrange("(o n) -> o n", o=1)
            act.wait_ge(centred, 1)
            for n in range(QUARTERS):
                act.wait_ge(centred, n + 1)
                t = quarter(n)
                act.activation(squares(t), H[:, t, :], ACT.Square).then_inc(squared, 1)
            for b in range(NB + 1):
                if b < NB:
                    turn_out(-1, b // 2, b % 2)
                if b:
                    project_out(-1, (b - 1) // 2, (b - 1) % 2)
                if b == 1:
                    act.wait_ge(vu_ready, 1)
                    act.dma_start(u_rows[0].rearrange("t p -> p t"), vu[:, 0:BT, 1], allow_slow_non_contiguous=True
                                  ).then_inc(u_first_stored, 16)
                if b == 4:
                    act.wait_ge(u_first_stored, 16)
                    act.dma_start(U[:, 0:BW], u_line[:, 0:BW].broadcast_to([P, BW])).then_inc(u_first_in, 16)
            act.wait_ge(vu_ready, NB)
            act.dma_start(u_rows[1:NB].rearrange("b t p -> p (b t)"), vu[:, BT:T, 1], allow_slow_non_contiguous=True
                          ).then_inc(u_rest_stored, 16)

            for layer in range(LAYERS):
                def group_signs(pair, u, g, layer=layer):
                    first = isinstance(pair, int) and (pair, u) == (0, 0)
                    if not (first and g < TSLOTS and layer == 0):
                        act.wait_ge(neg_ready, unit(layer, pair, u, g) - TSLOTS + 1)
                    act.sem_inc(act_passed, 1)
                    s8 = signs[:, g % TSLOTS, :].bitcast(I8)
                    for jj in range((FIRST_TILES if first else ACT_TILES)[layer]):
                        j = g * GT + jj
                        last = act.activation(s8[:, jj * BW:(jj + 1) * BW], urow(pair, u), ACT.Sign, bias=vc[:, j:j + 1])
                    last.then_inc(act_signs, 1)

                if layer:
                    act.wait_ge(u_in[0], urow_count(layer - 1, 0))
                else:
                    act.wait_ge(u_first_in, 16)
                act.wait_ge(vc_ready, layer + 1)
                group_signs(0, 0, 0)
                act.wait_ge(exps_in, 2 * layer + 1)
                act.activation(bd[:, :, :], bd[:, :, :], ACT.Exp).then_inc(bd_ready, 1)

                def signs_of(pair, u, layer=layer):
                    first = isinstance(pair, int) and pair == 0
                    if not (first and not u):
                        if layer:
                            act.wait_ge(u_in[u], urow_count(layer - 1, pair))
                        elif first:
                            act.wait_ge(u_rest_in, 16)
                    for g in range(NG):
                        n = layer * NG + g
                        if first and not u:
                            act.wait_ge(y_product, n + 1)
                            act.copy(parts(g * GT, (g + 1) * GT, 0), yf[:, g % 2, :, :, :]).then_inc(y_high, 1)
                        if not (first and not u and g == 0):
                            group_signs(pair, u, g)
                        if first and not u:
                            act.wait_ge(y_rest, n + 1)
                            act.copy(parts(g * GT, (g + 1) * GT, 1), yf[:, g % 2, :, :, :]).then_inc(y_mid, 1)
                            if g == 0:
                                act.wait_ge(exps_in, 2 * layer + 2)
                                act.activation(ac[:, :, :], ac[:, :, :], ACT.Exp).then_inc(ac_ready, 1)
                            if g == 4 and layer == 0:
                                act.wait_ge(u_rest_stored, 16)
                                act.dma_start(U[:, BW:N], u_line[:, BW:N].broadcast_to([P, N - BW])).then_inc(u_rest_in, 16)
                            if g == 1 and layer:
                                fetch(layer - 1, NB // 2 - 1, 0)
                            if g == 3 and layer:
                                fetch(layer - 1, NB // 2 - 1, 1)
                            continue
                        if layer and g == ELU_AT:
                            elu(*before(pair, u))
                        if g == ACT_TURN_AT and not first:
                            turn_out(layer, pair - 1, u)
                        if g == ACT_PROJ_AT and not first:
                            project_out(layer, pair - 1, u)
                        if g == ACT_FETCH_AT and not first and layer < 2:
                            fetch(layer, pair - 1, u)

                def elu(pair, u, half=None, layer=layer):
                    act.wait_ge(elu_in, nth(pair, u, half) + ((layer - 1) * (NB + 1) + 1))
                    act.activation(S[:, tt(half), 0, 0:C], num2[:, tt(half), 0:C], ACT.Exp).then_inc(elu_exp, 1)

                blocks(act, signs_of)
                turn_out(layer, NB // 2 - 1, 0)
                project_out(layer, NB // 2 - 1, 0)
                for half in range(2):
                    if layer:
                        elu(*LAST, half)
                    turn_out(layer, *LAST, half)
                    project_out(layer, *LAST, half)

        @block.vector
        def _(dve):
            chain = [0]

            def link(ins):
                chain[0] += 1
                ins.then_inc(dve_step, 1)
                dve.wait_ge(dve_step, chain[0])

            link(dve.memset(Wh[:, :, C:E1], 1.0))
            link(dve.memset(cc[:, 0:1], 0.0))

            def convert(pair, u, g):
                G = unit(0, pair, u, g)
                dve.wait_ge(adj_in[g % STAGES], (2 * pair + u) * 32 + 16 * (g // STAGES + 1))
                if u and g >= 2:
                    dve.wait_ge(edges_ready, pair * NG + (g - 1))
                to = oddbits[:, g % 2, :] if u else edges(pair, g)
                dve.tensor_scalar(to.bitcast(U8), stage(g % STAGES), 0.0, float(BIT[u]), ALU.is_gt, ALU.mult
                                  ).then_inc(stage_read, 1)

            def centre(n):
                t = quarter(n)
                dve.wait_ge(x_in[n], 16)
                link(dve.tensor_reduce(small[:, 0, t], X[:, t, :], AX.X, ALU.add))
                link(dve.tensor_scalar(small[:, 0, t], small[:, 0, t], 1.0 / C, None, ALU.mult))
                dve.tensor_tensor(H[:, t, :], X[:, t, :], wide(small[:, 0, t], C), ALU.subtract).then_inc(centred, 1)

            def variance(n):
                t = quarter(n)
                dve.wait_ge(squared, n + 1)
                link(dve.tensor_reduce(small[:, 1, t], squares(t), AX.X, ALU.add))
                dve.tensor_scalar(small[:, 1, t], small[:, 1, t], 1.0 / C, None, ALU.mult).then_inc(var_ready, 1)

            def scale(n):
                t = quarter(n)
                dve.wait_ge(rstd_ready, n + 1)
                dve.tensor_tensor(H[:, t, :], H[:, t, :], wide(small[:, 2, t], C), ALU.mult).then_inc(h_ready, NB // QUARTERS)

            centre(0)
            centre(1)
            dve.wait_ge(params_in, 16 * 9)
            dve.wait_ge(cleared, 3)
            for l in range(2):
                last = dve.tensor_scalar(linb_w[:, l, :], ones[0:HID, :], linb_sb[:, l:l + 1], None, ALU.mult)
            last.then_inc(cleared, 1)
            variance(0)
            centre(2)
            dve.wait_ge(prep_psum, 1)
            dve.tensor_copy(avu[:, 1:3, :], bank(1, 3)[0:C, 0:4].rearrange("p (l k) -> p l k", l=2))
            dve.tensor_copy(cc[:, 1:3], bank(1, 2)[:, 0:2]).then_inc(prep_copied, 1)
            scale(0)
            variance(1)
            dve.wait_ge(prep_psum, 2)
            dve.tensor_copy(rhs[:, :, C:C + 2], bank(0, 3)[0:C, 0:6].rearrange("p (l k) -> p l k", l=LAYERS)).then_inc(prep_copied, 1)
            centre(3)
            scale(1)
            variance(2)
            convert(0, 0, 0)
            variance(3)
            scale(2)
            convert(0, 0, 1)
            scale(3)

            for g in range(2, NG):
                convert(0, 0, g)

            signs_base = 0
            for layer in range(LAYERS):
                alpha = ALPHA[layer]
                dve.wait_ge(wh_ready, epi(layer, 0, 0))
                dve.reduce_max(vmax[:, :], vu[:, :, 0], AX.X).then_inc(part_max, 1)
                dve.tensor_scalar(vc[:, :], vu[:, :, 0], cc[:, layer:layer + 1], None, ALU.add)
                dve.tensor_scalar(nvc[:, :], vu[:, :, 0], cc[:, layer:layer + 1], -1.0, ALU.add, ALU.mult).then_inc(vc_ready, 1)
                dve.wait_ge(part_max_row, layer + 1)
                dve.reduce_max(vtop[:, :], bank(1, 0)[0:1, 0:P], AX.X).then_inc(top_ready, 1)
                def own_signs(pair, u, g, layer=layer):
                    tiles_of_act = (FIRST_TILES if isinstance(pair, int) and (pair, u) == (0, 0) else ACT_TILES)[layer]
                    if tiles_of_act == GT:
                        return
                    s8 = signs[:, g % TSLOTS, :].bitcast(U8)
                    for jj in range(tiles_of_act, GT):
                        j = g * GT + jj
                        last = dve.tensor_scalar(s8[:, jj * BW:(jj + 1) * BW], urow(pair, u), nvc[:, j:j + 1], float(BIT[0] | BIT[1]),
                                                 ALU.is_lt, ALU.mult)
                    last.then_inc(dve_signs, 1)

                if FIRST_TILES[layer] < GT:
                    if layer:
                        dve.wait_ge(u_in[0], urow_count(layer - 1, 0))
                    else:
                        dve.wait_ge(u_first_in, 16)
                    dve.wait_ge(vc_ready, layer + 1)
                    own_signs(0, 0, 0)
                dve.wait_ge(top_spread, layer + 1)
                link(dve.tensor_copy(V[:, :], bank(1, 1)[:, 0:1]))
                dve.tensor_scalar(bd[:, 0, :], vu[:, :, 0], V[:, :], SHIFT, ALU.subtract, ALU.add)
                link(dve.tensor_scalar(bd[:, 1, :], vu[:, :, 0], V[:, :], alpha, ALU.subtract, ALU.mult))
                dve.tensor_scalar(bd[:, 1, :], bd[:, 1, :], SHIFT, None, ALU.add).then_inc(exps_in, 1)
                def row_exponents(layer=layer, alpha=alpha, at=chain[0]):
                    dve.tensor_scalar(z[:, :], vu[:, :, 1], cc[:, layer:layer + 1], V[:, :], ALU.add, ALU.add).then_inc(dve_step, 1)
                    dve.wait_ge(dve_step, at + 1)
                    dve.tensor_scalar(az[:, :], z[:, :], alpha, None, ALU.mult).then_inc(dve_step, 1)
                    dve.wait_ge(dve_step, at + 2)
                    dve.tensor_tensor(zm[:, :], z[:, :], az[:, :], ALU.max).then_inc(dve_step, 1)
                    dve.wait_ge(dve_step, at + 3)
                    dve.tensor_tensor(ac[:, 0, :], z[:, :], zm[:, :], ALU.subtract)
                    dve.tensor_tensor(ac[:, 1, :], az[:, :], zm[:, :], ALU.subtract).then_inc(exps_in, 1)

                chain[0] += 3
                base = sum(ROW_STEPS[:layer]) * (NB + 1)
                per = ROW_STEPS[layer]

                row_steps = 12 if layer == 0 else 9

                def rows(s, pair, u, half=None, layer=layer, base=base, per=per):
                    if layer == 0 and half is None and s in POOL_STEPS:
                        return
                    n = nth(pair, u, half)
                    t = tt(half)
                    nt = t.stop - t.start
                    if s == 11:
                        dve.wait_ge(var_ready, QUARTERS + n + 1)
                    elif s:
                        dve.wait_ge(row_step, n * per + (base + s))
                    if s == 0:
                        if half == 0:
                            dve.wait_ge(half_used, layer + 1)
                        else:
                            dve.wait_ge(bits_used, unit(layer, pair, u, NG - 1) + 1)
                        dve.wait_ge(ac_ready, layer + 1)
                        for k in range(2):
                            last = dve.tensor_reduce(
                                S[:, t, k, :], ps[:, u, t, k * PARTS * E1:(k + 1) * PARTS * E1].rearrange("p t (q c) -> p t c q", q=PARTS),
                                AX.X, ALU.add)
                    elif s == 1:
                        ac4 = tiles(ac[:, :, :].rearrange("p k t -> p t k"), pair, u)[:, t, :]
                        last = dve.tensor_tensor(S[:, t, :, :], S[:, t, :, :], ac4.rearrange("p t (k o) -> p t k o", o=1).broadcast_to([P, nt, 2, E1]),
                                                 ALU.mult)
                    elif s == 2:
                        last = dve.tensor_tensor(num[:, t, :], S[:, t, 0, :], S[:, t, 1, :], ALU.add)
                    elif s == 3:
                        last = dve.tensor_scalar(small[:, 0, t], num[:, t, C], 0.0, None, ALU.is_equal)
                    elif s == 4:
                        dve.wait_ge(mean_ready, layer + 1)
                        last = dve.tensor_tensor(S[:, t, 0, :], mean[:, :].rearrange("p (o c) -> p o c", o=1).broadcast_to([P, nt, E1]),
                                                 wide(small[:, 0, t], E1), ALU.mult)
                    elif s == 5:
                        last = dve.tensor_tensor(num[:, t, :], num[:, t, :], S[:, t, 0, :], ALU.add)
                    elif s == 6:
                        last = dve.reciprocal(small[:, 3, t], num[:, t, C])
                    elif s == 7:
                        last = dve.tensor_tensor(num[:, t, 0:C], num[:, t, 0:C], wide(small[:, 3, t], C), ALU.mult)
                    elif layer:
                        dve.tensor_scalar(num2[:, t, 0:C], num[:, t, 0:C], 0.0, None, ALU.min).then_inc(elu_in, 1)
                        return
                    elif s == 8:
                        dve.wait_ge(x_added, 2)
                        last = dve.tensor_tensor(tiles(X, pair, u)[:, t, :], tiles(X, pair, u)[:, t, :], num[:, t, 0:C], ALU.add)
                    elif s == 9:
                        dve.sem_inc(dve_passed, 1)
                        for i in range(BT)[t]:
                            last = dve.bn_stats(stats[:, i, :], tiles(X, pair, u)[:, i, :])
                    elif s == 10:
                        dve.sem_inc(dve_passed, 1)
                        for i in range(BT)[t]:
                            last = dve.bn_aggr(mv[:, i, :], stats[:, i, :])
                        last.then_inc(var_ready, 1)
                        return
                    elif s == 11:
                        last = dve.tensor_tensor(num[:, t, 0:C], tiles(X, pair, u)[:, t, :], wide(mv[:, t, 0], C), ALU.subtract)
                    last.then_inc(row_step, 1)

                def next_h(pair, u, half=None, layer=layer, base=base, per=per):
                    n = nth(pair, u, half)
                    t = tt(half)
                    dve.wait_ge(turned, epi(layer, pair, u, half) - (back(half) - 1))
                    if layer == 0:
                        dve.wait_ge(rstd_ready, QUARTERS + n + 1)
                        if not (isinstance(pair, int) and pair == 0):
                            dve.wait_ge(h_kept, n - (back(half) - 1))
                        dve.wait_ge(row_step, n * per + (base + per))
                        dve.tensor_tensor(hn[:, buf(u, half), t, :], num[:, t, 0:C], wide(small[:, 2, t], C), ALU.mult).then_inc(h_ready, 1)
                    else:
                        dve.wait_ge(elu_exp, n + ((layer - 1) * (NB + 1) + 1))
                        dve.scalar_tensor_tensor(out=num[:, t, 0:C], in0=num[:, t, 0:C], scalar=0.0, in1=S[:, t, 0, 0:C],
                                                 op0=ALU.max, op1=ALU.add).then_inc(row_step, 1)
                        dve.wait_ge(row_step, n * per + (base + per))
                        dve.scalar_tensor_tensor(out=hn[:, buf(u, half), t, :], in0=num[:, t, 0:C], scalar=1.0 - MIX,
                                                 in1=tiles(H, pair, u)[:, t, :], op0=ALU.mult, op1=ALU.add).then_inc(h_ready, 1)

                def bits(pair, u, layer=layer, rows=rows, next_h=next_h, own_signs=own_signs,
                         signs_base=signs_base, row_steps=row_steps,
                         row_exponents=row_exponents):
                    first = isinstance(pair, int) and pair == 0
                    final = isinstance(pair, int) and pair == NB // 2 - 1
                    bit = BIT[u] * 0x01010101
                    own = (FIRST_TILES if first and not u else ACT_TILES)[layer] < GT
                    if layer == 0 and not u and not first:
                        dve.wait_ge(stage_read, unit(0, pair, u, NG - 1) + 1)
                    if own and not (first and not u):
                        dve.wait_ge(u_in[u], urow_count(layer - 1, pair))
                        own_signs(pair, u, 0)

                    def between(g, k):
                        at = 3 * g + k
                        if first and not u:
                            return
                        if 0 <= at - SPREAD_FROM < row_steps:
                            rows(at - SPREAD_FROM, *before(pair, u))
                        if at == NEXT_H_AT:
                            next_h(*before(pair, u))

                    def rest(g):
                        dve.wait_ge(y_high, layer * NG + g + 1)
                        dve.tensor_tensor(yf[:, g % 2, :, :, :], yf[:, g % 2, :, :, :], parts(g * GT, (g + 1) * GT, 0),
                                          ALU.subtract).then_inc(y_rest, 1)

                    def positive(g):
                        dve.wait_ge(neg_ready, unit(layer, pair, u, g) + 1)
                        s = slot_of(layer, pair, u, g)
                        dve.scalar_tensor_tensor(out=slot(s, 1), in0=edges(pair, g), scalar=bit, in1=slot(s, 0),
                                                 op0=ALU.bitwise_and, op1=ALU.bitwise_xor).then_inc(pos_ready, 1)

                    for g in range(NG):
                        G = unit(layer, pair, u, g)
                        s = slot_of(layer, pair, u, g)
                        start = first and not u and g == 0
                        if first and not u and g:
                            rest(g)
                        if layer == 0 and first and not u:
                            dve.wait_ge(stage_read, g + 1)
                        if own:
                            dve.wait_ge(dve_signs, (2 * pair + u) * NG + (signs_base + g + 1))
                        if layer == 0 and u:
                            dve.wait_ge(edges_ready, pair * NG + (g + 1))
                        dve.wait_ge(act_signs, G + 1)
                        if layer == 0 and is_last(pair, u) and g >= SLOTS[0]:
                            dve.wait_ge(stage_read, NB * NG)
                        elif not (first and not u and g < SLOTS[layer]):
                            dve.wait_ge(bits_used, G - SLOTS[layer] + 1)
                        dve.scalar_tensor_tensor(out=slot(s, 0), in0=edges(pair, g), scalar=bit, in1=signs[:, g % TSLOTS, :],
                                                 op0=ALU.bitwise_and, op1=ALU.bitwise_and).then_inc(neg_ready, 1)
                        between(g, 0)
                        if start:
                            positive(g)
                            rest(g)
                            row_exponents()
                        if g + 1 < NG:
                            own_signs(pair, u, g + 1)
                        if layer == 0 and not (final and u):
                            convert(pair + u, 1 - u, g)
                        between(g, 1)
                        if not start:
                            positive(g)
                        if first and not u:
                            if g == NG - 1:
                                dve.wait_ge(mean_psum, layer + 1)
                                dve.tensor_copy(mean[:, :], bank(1, 2)[:, 0:E1]).then_inc(mean_ready, 1)
                        between(g, 2)

                blocks(dve, bits, peel_last=layer == 0)
                for half in range(2):
                    for s in range(row_steps):
                        rows(s, *LAST, half)
                    next_h(*LAST, half)
                signs_base += NG * (NB if ACT_TILES[layer] < GT else int(FIRST_TILES[layer] < GT))


def kernel(**inputs):
    import numpy as np
    import concourse.bacc as bacc
    from concourse import mybir as mb
    from concourse.bass_utils import run_bass_kernel_spmd

    a = {k: np.asarray(v) for k, v in inputs.items()}
    adj = a["adj"].reshape(P, NB, BT, P, NG, GT).transpose(1, 4, 3, 5, 2, 0).reshape(NB * NG, P, GT * BW)
    w = np.stack([a["L0_gnn_weight_w"], a["L1_gnn_W"][0], a["L1_gnn_W"][1]])
    arrays = {
        "x": a["x"],
        "adj": adj,
        "bias0": np.broadcast_to(a["L0_gnn_bias"], (P, C)),
        "mlp_b": np.broadcast_to(a["L1_gnn_mlp_b"], (P, C)),
        "w": w.transpose(1, 0, 2),
        "wT": w.transpose(2, 0, 1),
        "a0": a["L0_gnn_weight_a"].reshape(2, C)[::-1].T,
        "lT": a["L1_gnn_lin_w"].reshape(2, 2, C, HID).transpose(3, 0, 1, 2),
        "attn": a["L1_gnn_attn"][:, :, 0].T,
        "lin_b": a["L1_gnn_lin_b"].T,
        "mlp_w": a["L1_gnn_mlp_w"].reshape(LAYERS, C, C)[[2, 0, 1]].transpose(1, 0, 2),
    }
    nc = bacc.Bacc("TRN2", target_bir_lowering=False, num_devices=1)
    sent, args = {}, []
    for name, value in arrays.items():
        value = np.ascontiguousarray(value)
        sent[f"{name}_dram"] = value
        args.append(nc.dram_tensor(f"{name}_dram", value.shape, mb.dt.from_np(value.dtype), kind="ExternalInput").ap())
    out = nc.dram_tensor("out_dram", (N, C), mb.dt.float32, kind="ExternalOutput").ap()
    u_rows = nc.dram_tensor("u_rows_dram", (NB, BT, P), mb.dt.float32, kind="Internal").ap()
    build(nc, *args, u_rows, out)
    r = run_bass_kernel_spmd(nc, [sent], core_ids=[0])
    return r.results[0]["out_dram"]
```
